# Optimizing a Trainium2 kernel written in Bass

```python
import numpy as np
import jax
import jax.numpy as jnp

def _softmax(x, axis=-1):
    return jax.nn.softmax(x, axis=axis)

def _gelu(x):
    return jax.nn.gelu(x, approximate=True)

def _silu(x):
    return jax.nn.silu(x)

def _sigmoid(x):
    return jax.nn.sigmoid(x)

def _layernorm(x, axis=-1, eps=1e-05):
    m = jnp.mean(x, axis=axis, keepdims=True)
    v = jnp.var(x, axis=axis, keepdims=True)
    return (x - m) / jnp.sqrt(v + eps)

def _scatter_add(tgt, idx, src, axis=0):
    return tgt.at[idx].add(src)

def _segment_sum(src, seg, n):
    return jax.ops.segment_sum(src, seg, n)
kernel_name = 'mk_macaron_d1_jaxref_r8_ceed17'

def setup_inputs(seed: int=0):
    np.random.seed(seed)
    _w = jnp.asarray

    def _L0_attn_setup():
        import jax, jax.numpy as jnp
        import numpy as np
        D_MODEL = 128
        N_HEADS = 32
        HEAD_DIM = D_MODEL // N_HEADS
        EPS = 1e-05
        key = jax.random.key(seed)
        ks = jax.random.split(key, 6)
        B, S = (2, 256)
        scale = 1.0 / np.sqrt(D_MODEL)
        return {'x': jax.random.normal(ks[0], (B, S, D_MODEL), dtype=jnp.float32), 'Wqkv_w': jax.random.normal(ks[1], (3 * D_MODEL, D_MODEL), dtype=jnp.float32) * scale, 'Wqkv_b': jax.random.normal(ks[2], (3 * D_MODEL,), dtype=jnp.float32) * 0.01, 'gn_w': jnp.ones((D_MODEL,), dtype=jnp.float32), 'gn_b': jnp.zeros((D_MODEL,), dtype=jnp.float32), 'out_w': jax.random.normal(ks[3], (D_MODEL, D_MODEL), dtype=jnp.float32) * scale, 'out_b': jax.random.normal(ks[4], (D_MODEL,), dtype=jnp.float32) * 0.01}
    _L0_attn_in = _L0_attn_setup()

    def _L0_ffn_setup():
        import jax, jax.numpy as jnp
        import numpy as np
        B, S, D = (1, 256, 128)
        E, F = (16, 128)
        NG, TKG, K = (4, 2, 4)
        NSH = 2
        SCALE = 2.5
        STD = 0.02
        EPG = E // NG

        def _route(x_flat, router_w, bias):
            logits = x_flat.astype(jnp.float32) @ router_w.T
            scores = jax.nn.sigmoid(logits)
            s = scores + bias[None, :]
            sg = s.reshape(-1, NG, EPG)
            group_score = jax.lax.top_k(sg, 2)[0].sum(-1)
            gidx = jax.lax.top_k(group_score, TKG)[1]
            gmask = jnp.sum(jax.nn.one_hot(gidx, NG, dtype=jnp.float32), axis=1) > 0
            emask = jnp.repeat(gmask, EPG, axis=1)
            masked = jnp.where(emask, s, -1.0)
            topk_idx = jax.lax.top_k(masked, K)[1]
            tw = jnp.take_along_axis(scores, topk_idx, axis=1)
            tw = tw / (tw.sum(-1, keepdims=True) + 1e-20)
            tw = tw * SCALE
            return (topk_idx, tw)
        key = jax.random.key(seed)
        ks = jax.random.split(key, 8)
        return {'hidden_states': jax.random.normal(ks[0], (B, S, D), jnp.float32), 'router_w': jax.random.normal(ks[1], (E, D), jnp.float32) * STD, 'bias': jnp.zeros((E,), jnp.float32), 'gate_w': jax.random.normal(ks[2], (E, D, F), jnp.float32) * STD, 'up_w': jax.random.normal(ks[3], (E, D, F), jnp.float32) * STD, 'down_w': jax.random.normal(ks[4], (E, F, D), jnp.float32) * STD, 'sh_gate_w': jax.random.normal(ks[5], (D, NSH * F), jnp.float32) * STD, 'sh_up_w': jax.random.normal(ks[6], (D, NSH * F), jnp.float32) * STD, 'sh_down_w': jax.random.normal(ks[7], (NSH * F, D), jnp.float32) * STD}
    _L0_ffn_in = _L0_ffn_setup()
    _d = {'L0_attn_x': _L0_attn_in['x'], 'L0_attn_Wqkv_w': _L0_attn_in['Wqkv_w'], 'L0_attn_Wqkv_b': _L0_attn_in['Wqkv_b'], 'L0_attn_gn_w': _L0_attn_in['gn_w'], 'L0_attn_gn_b': _L0_attn_in['gn_b'], 'L0_attn_out_w': _L0_attn_in['out_w'], 'L0_attn_out_b': _L0_attn_in['out_b'], 'L0_ffn_router_w': _L0_ffn_in['router_w'], 'L0_ffn_bias': _L0_ffn_in['bias'], 'L0_ffn_gate_w': _L0_ffn_in['gate_w'], 'L0_ffn_up_w': _L0_ffn_in['up_w'], 'L0_ffn_down_w': _L0_ffn_in['down_w'], 'L0_ffn_sh_gate_w': _L0_ffn_in['sh_gate_w'], 'L0_ffn_sh_up_w': _L0_ffn_in['sh_up_w'], 'L0_ffn_sh_down_w': _L0_ffn_in['sh_down_w']}
    _x0 = _d['L0_attn_x']
    _d['L0_attn_x'] = jax.random.normal(jax.random.fold_in(jax.random.key(seed), 1), (4, 1024, 128), dtype=_x0.dtype)
    del _x0
    return _d

def reference(L0_attn_x, L0_attn_Wqkv_w, L0_attn_Wqkv_b, L0_attn_gn_w, L0_attn_gn_b, L0_attn_out_w, L0_attn_out_b, L0_ffn_router_w, L0_ffn_bias, L0_ffn_gate_w, L0_ffn_up_w, L0_ffn_down_w, L0_ffn_sh_gate_w, L0_ffn_sh_up_w, L0_ffn_sh_down_w):

    def _L0_attn_ref(x, Wqkv_w, Wqkv_b, gn_w, gn_b, out_w, out_b):
        import jax, jax.numpy as jnp
        import numpy as np
        D_MODEL = 128
        N_HEADS = 32
        HEAD_DIM = D_MODEL // N_HEADS
        EPS = 1e-05
        B, S, Dm = x.shape
        H, Dh = (N_HEADS, HEAD_DIM)
        qkv = x @ Wqkv_w.T + Wqkv_b
        qkv = qkv.reshape(B, S, 3, H, Dh)
        q, k, v = (qkv[:, :, 0], qkv[:, :, 1], qkv[:, :, 2])
        a = jnp.einsum('bthd,bshd->bhts', q, k)
        ctx = jnp.einsum('bhts,bshd->bthd', a, v)
        g = ctx.transpose(0, 2, 3, 1)
        mean = g.mean(axis=(2, 3), keepdims=True)
        var = ((g - mean) ** 2).mean(axis=(2, 3), keepdims=True)
        gh = (g - mean) * jax.lax.rsqrt(var + EPS)
        gh = gh * gn_w.reshape(H, Dh, 1) + gn_b.reshape(H, Dh, 1)
        ctx = gh.transpose(0, 3, 1, 2).reshape(B, S, Dm)
        return ctx @ out_w.T + out_b

    def _L0_ffn_ref(hidden_states, router_w, bias, gate_w, up_w, down_w, sh_gate_w, sh_up_w, sh_down_w):
        import jax, jax.numpy as jnp
        import numpy as np
        B, S, D = (1, 256, 128)
        E, F = (16, 128)
        NG, TKG, K = (4, 2, 4)
        NSH = 2
        SCALE = 2.5
        STD = 0.02
        EPG = E // NG

        def _route(x_flat, router_w, bias):
            logits = x_flat.astype(jnp.float32) @ router_w.T
            scores = jax.nn.sigmoid(logits)
            s = scores + bias[None, :]
            sg = s.reshape(-1, NG, EPG)
            group_score = jax.lax.top_k(sg, 2)[0].sum(-1)
            gidx = jax.lax.top_k(group_score, TKG)[1]
            gmask = jnp.sum(jax.nn.one_hot(gidx, NG, dtype=jnp.float32), axis=1) > 0
            emask = jnp.repeat(gmask, EPG, axis=1)
            masked = jnp.where(emask, s, -1.0)
            topk_idx = jax.lax.top_k(masked, K)[1]
            tw = jnp.take_along_axis(scores, topk_idx, axis=1)
            tw = tw / (tw.sum(-1, keepdims=True) + 1e-20)
            tw = tw * SCALE
            return (topk_idx, tw)
        x = hidden_states.reshape(-1, D)
        topk_idx, tw = _route(x, router_w, bias)
        combine = (jax.nn.one_hot(topk_idx, E, dtype=tw.dtype) * tw[..., None]).sum(1)
        h = jnp.einsum('td,edf->etf', x, gate_w)
        u = jnp.einsum('td,edf->etf', x, up_w)
        y = jnp.einsum('etf,efd->etd', jax.nn.silu(h) * u, down_w)
        routed = jnp.einsum('etd,te->td', y, combine)
        sh = jax.nn.silu(x @ sh_gate_w) * (x @ sh_up_w) @ sh_down_w
        return (routed + sh).reshape(hidden_states.shape)
    x = L0_attn_x
    x = x + 0.5 * _L0_ffn_ref(_layernorm(x, axis=-1), L0_ffn_router_w, L0_ffn_bias, L0_ffn_gate_w, L0_ffn_up_w, L0_ffn_down_w, L0_ffn_sh_gate_w, L0_ffn_sh_up_w, L0_ffn_sh_down_w)
    x = x + _L0_attn_ref(_layernorm(x, axis=-1), L0_attn_Wqkv_w, L0_attn_Wqkv_b, L0_attn_gn_w, L0_attn_gn_b, L0_attn_out_w, L0_attn_out_b)
    x = x + 0.5 * _L0_ffn_ref(_layernorm(x, axis=-1), L0_ffn_router_w, L0_ffn_bias, L0_ffn_gate_w, L0_ffn_up_w, L0_ffn_down_w, L0_ffn_sh_gate_w, L0_ffn_sh_up_w, L0_ffn_sh_down_w)
    return x

_drawn_inputs = setup_inputs


def setup_inputs(seed=0):
    import zlib

    import numpy as np

    out = dict(_drawn_inputs(seed))
    spreads = {'L0_attn_gn_w': (1.0, 0.2), 'L0_attn_gn_b': (0.0, 0.1), 'L0_ffn_bias': (0.0, 0.8)}
    factors = {'L0_attn_Wqkv_b': 8.0,
     'L0_attn_out_b': 7.93,
     'L0_ffn_router_w': 8.0,
     'L0_ffn_gate_w': 8.0,
     'L0_ffn_up_w': 8.0,
     'L0_ffn_down_w': 8.0,
     'L0_ffn_sh_gate_w': 8.0,
     'L0_ffn_sh_up_w': 8.0,
     'L0_ffn_sh_down_w': 8.0}
    for name, (base, spread) in spreads.items():
        noise = np.random.default_rng([zlib.crc32(name.encode()), seed]).standard_normal(out[name].shape)
        drawn = base * np.exp(spread * noise) if base else spread * noise
        out[name] = jnp.asarray(drawn.astype(out[name].dtype))
    for name, factor in factors.items():
        out[name] = (out[name] * factor).astype(out[name].dtype)
    return out
```

```python
from contextlib import ExitStack

import concourse.bass as bass
from concourse import mybir

F32 = mybir.dt.float32
F32R = mybir.dt.float32r
U32 = mybir.dt.uint32
ALU = mybir.AluOpType
ACT = mybir.ActivationFunctionType
AX = mybir.AxisListType

P = 128
HEAD = 4
EPS = 1e-5
GROUPS, PER_GROUP = 4, 4
TOP_GROUPS, TOP_K = 2, 4
ROUTED_SCALE = 2.5
SHARED = 2
BLOCK = 512
TILES = BLOCK // P
NEAR_ZERO = 2.0 ** -24


def macaron_kernel(nc, x, Wqkv_w, Wqkv_b, gn_w, gn_b, out_w, out_b, router_w, bias,
                   gate_w, up_w, down_w, sh_gate_w, sh_up_w, sh_down_w, out):
    BATCH, SEQ, D = x.shape
    E = router_w.shape[0]
    UNITS = SHARED + E
    PAIR = 2 * UNITS
    BT = SEQ // P
    NBLK = BATCH * SEQ // BLOCK
    STEPS = 2 * NBLK
    PAIRS = STEPS // 2
    LAST = PAIRS - 1
    ATT0, ATT1 = 1, BATCH + 1
    LAG = 3
    ESEM = 4
    ROUTE_OPS = 27
    CONSTS = 12
    ATT_OPS = 21
    assert D == P and BT * P == SEQ and NBLK == 2 * BATCH and E == GROUPS * PER_GROUP

    x_v = x.rearrange("b (p j) d -> b p j d", j=BT)
    out_v = out.rearrange("b (p h j) d -> b h p j d", h=2, j=TILES)

    ctx = ExitStack()
    with ctx:
        def sb(name, shape, dt=F32):
            return ctx.enter_context(nc.sbuf_tensor(name, shape, dt))

        def pb(name):
            return ctx.enter_context(nc.psum_tensor(name, [P, 512], F32))

        def sem(name):
            return ctx.enter_context(nc.semaphore(name))

        X = sb("X", [P, BATCH * BT, P])
        W_in = sb("W_in", [P, UNITS, 3, P])
        W_hi = sb("W_hi", [P, UNITS, 3, P], F32R)
        W_lo = sb("W_lo", [P, UNITS, 3, P], F32R)
        XT_hi = sb("XT_hi", [P, 2, BLOCK], F32R)
        XT_lo = sb("XT_lo", [P, 2, BLOCK], F32R)
        S = sb("S", [P, 2, BLOCK])
        SU = sb("SU", [P, 2, BLOCK])
        A = sb("A", [P, 3, BLOCK])
        A_hi = sb("A_hi", [P, 3, BLOCK], F32R)
        A_lo = sb("A_lo", [P, 3, BLOCK], F32R)
        CB = sb("CB", [P, E, BLOCK])
        YT = sb("YT", [P, BLOCK])
        bst = sb("bst", [P, TILES, 6])
        parts = sb("parts", [P, 5, TILES])
        mean = sb("mean", [P, TILES])
        vareps = sb("vareps", [P, TILES])
        rstd = sb("rstd", [P, TILES])
        XN = sb("XN", [P, TILES, P])
        lg = sb("lg", [P, TILES, E])
        near = sb("near", [P, TILES, E])
        sil = sb("sil", [P, TILES, E])
        rcl = sb("rcl", [P, TILES, E])
        score = sb("score", [P, TILES, E])
        sel = sb("sel", [P, TILES, E])
        hi2 = sb("hi2", [P, TILES * GROUPS, 2])
        lo2 = sb("lo2", [P, TILES * GROUPS, 2])
        top1 = sb("top1", [P, TILES * GROUPS])
        mid = sb("mid", [P, TILES * GROUPS])
        low1 = sb("low1", [P, TILES * GROUPS])
        gsc = sb("gsc", [P, TILES, GROUPS])
        gt = sb("gt", [P, TILES, GROUPS, GROUPS])
        eq = sb("eq", [P, TILES, GROUPS, GROUPS])
        grank = sb("grank", [P, TILES * GROUPS])
        gmask = sb("gmask", [P, TILES * GROUPS])
        picked = sb("picked", [P, TILES, E])
        masked = sb("masked", [P, TILES, E])
        top8 = sb("top8", [P, TILES, 8])
        idx8 = sb("idx8", [P, TILES, 8], U32)
        hot = sb("hot", [P, TILES, E, TOP_K])
        emask = sb("emask", [P, TILES, E])
        wsel = sb("wsel", [P, TILES, E])
        wsum = sb("wsum", [P, TILES])
        wrec = sb("wrec", [P, TILES])
        comb = sb("comb", [P, TILES, E])
        CT = sb("CT", [E, BLOCK])
        ones = sb("ones", [P, P])
        ident = sb("ident", [P, P])
        half = sb("half", [P, BT])
        before = sb("before", [P, TILES, GROUPS, GROUPS])
        enum = sb("enum", [P, TILES, E, TOP_K])
        blk1 = sb("blk1", [P, P])
        blkm = sb("blkm", [P, P])
        R_in = sb("R_in", [E, P])
        RT_hi = sb("RT_hi", [P, E], F32R)
        RT_lo = sb("RT_lo", [P, E], F32R)
        ebias = sb("ebias", [P, TILES, E])
        Wq = sb("Wq", [P, P + 1])
        Wk_in = sb("Wk_in", [P, P])
        Wv_in = sb("Wv_in", [P, P])
        Wo_in = sb("Wo_in", [P, P])
        WkT = sb("WkT", [P, P])
        WvT = sb("WvT", [P, P])
        WoT = sb("WoT", [P, P])
        bk = sb("bk", [P, 1])
        bvb = sb("bvb", [P, P])
        bob = sb("bob", [P, P])
        gw = sb("gw", [P, 1])
        gb = sb("gb", [P, 1])
        ast = sb("ast", [P, BT, 6])
        aparts = sb("aparts", [P, 5, BT])
        amean = sb("amean", [P, BT])
        avar = sb("avar", [P, BT])
        arstd = sb("arstd", [P, BT])
        XA = sb("XA", [P, BT, P + 1])
        XAT = sb("XAT", [P, BT, P])
        GS = sb("GS", [P, P + 1])
        s_row = sb("s_row", [P, P])
        nmu = sb("nmu", [P, 1])
        P1 = sb("P1", [P, P])
        rv = sb("rv", [P, P])
        Gn = sb("Gn", [P, P])
        Gc = sb("Gc", [P, P + 1])
        Mf = sb("Mf", [P, P])
        Mm = sb("Mm", [P, P])
        AT = sb("AT", [P, P + 1])
        Am = sb("Am", [P, P])
        quad = sb("quad", [P, P])
        chvar = sb("chvar", [P, 1])
        chmean = sb("chmean", [P, 1])
        dev = sb("dev", [P, 1])
        dev2 = sb("dev2", [P, 1])
        gvar = sb("gvar", [P, 1])
        gmean = sb("gmean", [P, 1])
        grstd = sb("grstd", [P, 1])
        gsc1 = sb("gsc1", [P, 1])
        gms = sb("gms", [P, 1])
        gsh = sb("gsh", [P, 1])
        z1 = sb("z1", [P, 1])
        zb = sb("zb", [P, P])
        ATs = sb("ATs", [P, P])
        Bm = sb("Bm", [P, P])
        brow = sb("brow", [P, P])

        gateP = [pb("gateP0"), pb("gateP1")]
        upP = [pb("upP0"), pb("upP1")]
        yP = pb("yP")
        prepP = pb("prepP")
        backP = pb("backP")
        attP = pb("attP")

        combT = nc.dram_tensor("combT", [STEPS, E, BLOCK], F32, kind="Internal").ap()

        x_first, x_rest = sem("x_first"), sem("x_rest")
        w_in = [sem(f"w_in{i}") for i in range(1 + E // ESEM)]
        small_in = sem("small_in")
        const_seq = sem("const_seq")
        w_hi_done, w_lo_done = sem("w_hi_done"), sem("w_lo_done")
        setup_psum, setup_sb = sem("setup_psum"), sem("setup_sb")
        gate_done, up_done, down_done = sem("gate_done"), sem("up_done"), sem("down_done")
        silu_done, mul_done, weighted = sem("silu_done"), sem("mul_done"), sem("weighted")
        high_done, low_done = sem("high_done"), sem("low_done")
        y_copied, y_back, x_updated = sem("y_copied"), sem("y_back"), sem("x_updated")
        stats_seq, rstd_ready, xn_ready = sem("stats_seq"), sem("rstd_ready"), sem("xn_ready")
        xt_done, xt_hi_ready, xt_lo_ready = sem("xt_done"), sem("xt_hi_ready"), sem("xt_lo_ready")
        logits_done, silu_route, route_seq = sem("logits_done"), sem("silu_route"), sem("route_seq")
        norm_seq = sem("norm_seq")
        z_ready, row_added = sem("z_ready"), sem("row_added")
        ct_done, ct_ready, ct_stored = sem("ct_done"), sem("ct_ready"), sem("ct_stored")
        cb_in = [sem(f"cb_in{i}") for i in range(E // ESEM)]
        stored = sem("stored")
        att_seq = sem("att_seq")
        att_pow = sem("att_pow")
        att_pe = sem("att_pe")
        att_act = sem("att_act")
        attended = sem("attended")

        block = ctx.enter_context(nc.Block())

        def mod(p, m):
            return p % m

        @block.sync
        def _(sp):
            sp.dma_start(X[:, 0:TILES, :], x_v[0][:, 0:TILES, :]).then_inc(x_first, 16)
            for i, w in enumerate((sh_gate_w, sh_up_w)):
                sp.dma_start(W_in[:, 0:SHARED, i, :],
                             w.rearrange("d (s f) -> d s f", s=SHARED)).then_inc(w_in[0], 16)
            sp.dma_start(W_in[:, 0:SHARED, 2, :],
                         sh_down_w.rearrange("(s f) d -> f s d", s=SHARED)).then_inc(w_in[0], 16)
            for g in range(E // ESEM):
                for i, w in enumerate((gate_w, up_w, down_w)):
                    sp.dma_start(W_in[:, SHARED + g * ESEM:SHARED + (g + 1) * ESEM, i, :],
                                 w[g * ESEM:(g + 1) * ESEM].rearrange("e k m -> k e m")
                                 ).then_inc(w_in[1 + g], 16)
                if g == 0:
                    sp.dma_start(X[:, TILES:BT, :], x_v[0][:, TILES:BT, :]).then_inc(x_rest, 16)
            for b in range(1, BATCH):
                sp.dma_start(X[:, b * BT:(b + 1) * BT, :], x_v[b]).then_inc(x_rest, 16)

            def spread_weights(t, first):
                sp.wait_ge(ct_ready, t + 1)
                sp.dma_start(combT[bass.ds(t, 1)].rearrange("o e n -> (o e) n"),
                             CT[:, :]).then_inc(ct_stored, 16)
                sp.wait_ge(ct_stored, 16 * (t + 1))
                for g in range(E // ESEM):
                    if not first:
                        sp.wait_ge(weighted, E * (t - 1) + (g + 1) * ESEM)
                    src = combT[bass.ds(t, 1), g * ESEM:(g + 1) * ESEM, :]
                    sp.dma_start(CB[:, g * ESEM:(g + 1) * ESEM, :],
                                 src.broadcast_to([P, ESEM, BLOCK])).then_inc(cb_in[g], 16)

            def store(t):
                sp.wait_ge(x_updated, t + 1)
                blk = t - NBLK
                dst = out_v[bass.ds(blk // 2, 1), bass.ds(blk % 2, 1)]
                sp.dma_start(dst.rearrange("b h p j d -> (b h p) j d"),
                             X[:, bass.ds(blk * TILES, TILES), :]).then_inc(stored, 16)

            spread_weights(0, True)
            with sp.Fori(1, NBLK + 1) as t:
                spread_weights(t, False)
            with sp.Fori(NBLK + 1, STEPS) as t:
                spread_weights(t, False)
                store(t - 1)
            store(STEPS - 1)
            sp.wait_ge(stored, 16 * NBLK)

        @block.gpsimd
        def _(pool):
            for dst, src in ((R_in[:, :], router_w),
                             (Wq[:, 0:P], Wqkv_w[0:P]),
                             (Wq[:, P:P + 1], Wqkv_b[0:P].unsqueeze(1)),
                             (Wk_in[:, :], Wqkv_w[P:2 * P]),
                             (Wv_in[:, :], Wqkv_w[2 * P:3 * P]),
                             (Wo_in[:, :], out_w),
                             (bk[:, :], Wqkv_b[P:2 * P].unsqueeze(1)),
                             (gw[:, :], gn_w.unsqueeze(1)),
                             (gb[:, :], gn_b.unsqueeze(1)),
                             (bvb[:, :], Wqkv_b[2 * P:3 * P].unsqueeze(0).broadcast_to([P, P])),
                             (bob[:, :], out_b.unsqueeze(0).broadcast_to([P, P])),
                             (ebias[:, :, :], bias.unsqueeze(0).unsqueeze(0).broadcast_to([P, TILES, E]))):
                pool.dma_start(dst, src).then_inc(small_in, 16)
            pool.memset(ident[:, :], 0.0).then_inc(const_seq, 1)
            pool.memset(half[:, :], -0.5).then_inc(const_seq, 1)
            pool.memset(ones[:, :], 1.0).then_inc(const_seq, 1)
            pool.wait_ge(const_seq, 1)
            pool.affine_select(out=ident[:, :], in_=ident[:, :], compare_op=ALU.not_equal, fill=1.0,
                               base=0, pattern=[[-1, P]], channel_multiplier=1).then_inc(const_seq, 1)
            pool.memset(before[:, :, :, :], 1.0).then_inc(const_seq, 1)
            pool.memset(XA[:, :, :], 1.0).then_inc(const_seq, 1)
            pool.memset(blk1[:, :], 1.0).then_inc(const_seq, 1)
            pool.memset(Gc[:, :], 0.0).then_inc(const_seq, 1)
            pool.iota(enum[:, :, :, :], pattern=[[0, TILES], [1, E], [0, TOP_K]], base=0,
                      channel_multiplier=0, allow_small_or_imprecise_dtypes=True).then_inc(const_seq, 1)
            pool.wait_ge(const_seq, 9)
            pool.affine_select(out=before[:, :, :, :], in_=before[:, :, :, :], compare_op=ALU.is_ge,
                               fill=0.0, base=-1, pattern=[[0, TILES], [1, GROUPS], [-1, GROUPS]],
                               channel_multiplier=0).then_inc(const_seq, 1)
            heads = blk1[:, :].rearrange("p (h c) -> p h c", c=HEAD)
            pool.affine_select(out=heads, in_=heads, compare_op=ALU.is_ge, fill=0.0, base=0,
                               pattern=[[-HEAD, P // HEAD], [0, HEAD]],
                               channel_multiplier=1).then_inc(const_seq, 1)
            pool.wait_ge(const_seq, 11)
            pool.affine_select(out=heads, in_=heads, compare_op=ALU.is_ge, fill=0.0, base=HEAD - 1,
                               pattern=[[HEAD, P // HEAD], [0, HEAD]],
                               channel_multiplier=-1).then_inc(const_seq, 1)

            def split_low(unit):
                pool.wait_ge(w_hi_done, unit + 1)
                pool.tensor_tensor(W_lo[:, unit, :, :], W_in[:, unit, :, :],
                                   W_hi[:, unit, :, :].bitcast(F32),
                                   ALU.subtract).then_inc(w_lo_done, 1)

            def step_rstd(t):
                pool.wait_ge(stats_seq, 4 * (t + 1))
                pool.tensor_tensor(rstd[:, :], vareps[:, :], half[:, 0:TILES],
                                   ALU.pow).then_inc(rstd_ready, 1)

            def pair(p, first, attention, last):
                n = PAIR * p
                for u in range(PAIR):
                    w, s = u % UNITS, u // UNITS
                    if first and u + LAG < UNITS:
                        split_low(u + LAG)
                    if w == 1 and not (last and s == 1):
                        step_rstd(2 * p + s + 1)
                    if attention and u == 10:
                        pool.wait_ge(att_seq, ATT_OPS * (p - ATT0) + 4)
                        pool.tensor_tensor(arstd[:, :], avar[:, :], half[:, :],
                                           ALU.pow).then_inc(att_pow, 1)
                    if attention and u == 28:
                        pool.wait_ge(att_seq, ATT_OPS * (p - ATT0) + 16)
                        pool.tensor_tensor(grstd[:, :], gvar[:, :], half[:, 0:1],
                                           ALU.pow).then_inc(att_pow, 1)
                    pool.wait_ge(high_done, n + u + 1)
                    pool.tensor_tensor(A_lo[:, u % 3, :], A[:, u % 3, :],
                                       A_hi[:, u % 3, :].bitcast(F32),
                                       ALU.subtract).then_inc(low_done, 1)

            step_rstd(0)
            for unit in range(LAG):
                split_low(unit)
            pair(0, True, False, False)
            with pool.Fori(ATT0, ATT1) as p:
                pair(p, False, True, False)
            with pool.Fori(ATT1, LAST) as p:
                pair(p, False, False, False)
            pair(LAST, False, False, True)

        @block.tensor
        def _(pe):
            def product(dst, hi_w, lo_w, hi_x, lo_x, start, stop):
                pe.matmul(dst, hi_w, hi_x, start=start, stop=False)
                pe.matmul(dst, lo_w, hi_x, start=False, stop=False)
                return pe.matmul(dst, hi_w, lo_x, start=False, stop=stop)

            def down(n, u, t):
                w = u % UNITS
                if w == 0 and not (isinstance(t, int) and t == 0):
                    pe.wait_ge(y_copied, t)
                pe.wait_ge(low_done, n + u + 1)
                product(yP[:, :], W_hi[:, w, 2, :], W_lo[:, w, 2, :], A_hi[:, u % 3, :],
                        A_lo[:, u % 3, :], w == 0, w == UNITS - 1).then_inc(down_done, 1)

            def transpose_back(t):
                pe.wait_ge(y_copied, t + 1)
                for j in range(TILES):
                    mm = pe.transpose(backP[:, j * P:(j + 1) * P], YT[:, j * P:(j + 1) * P], ident[:, :])
                mm.then_inc(y_back, 1)

            def transpose_next(t):
                pe.wait_ge(xn_ready, t + 1)
                for j in range(TILES):
                    mm = pe.transpose(prepP[:, j * P:(j + 1) * P], XN[:, j, :], ident[:, :])
                mm.then_inc(xt_done, 1)

            def logits(t, q):
                pe.wait_ge(xt_lo_ready, t + 1)
                for j in range(TILES):
                    hi, lo = XT_hi[:, q, j * P:(j + 1) * P], XT_lo[:, q, j * P:(j + 1) * P]
                    mm = product(prepP[:, j * E:(j + 1) * E], hi, lo, RT_hi[:, :], RT_lo[:, :], True, True)
                mm.then_inc(logits_done, 1)

            def transpose_weights(t):
                pe.wait_ge(route_seq, ROUTE_OPS * (t + 1))
                for j in range(TILES):
                    mm = pe.transpose(prepP[0:E, j * P:(j + 1) * P], comb[:, j, :], ident[:, :])
                mm.then_inc(ct_done, 1)

            def attention_stage(u, b):
                v = ATT_OPS * b
                if u in (12, 14):
                    g = (u - 12) // 2
                    if g == 0:
                        pe.wait_ge(att_seq, v + 5)
                    else:
                        pe.wait_ge(att_act, 6 * b + 1)
                    for j in range(TILES):
                        mm = pe.transpose(attP[:, j * P:(j + 1) * P], XA[:, g * TILES + j, 0:P], ident[:, :])
                    mm.then_inc(att_pe, 1)
                if u == 16:
                    pe.wait_ge(att_act, 6 * b + 2)
                    for j in range(BT):
                        mm = pe.matmul(attP[:, 0:P + 1], XA[:, j, 0:P], XA[:, j, :],
                                       start=(j == 0), stop=(j == BT - 1))
                    mm.then_inc(att_pe, 1)
                if u == 18:
                    pe.wait_ge(att_act, 6 * b + 3)
                    pe.wait_ge(att_seq, v + 6)
                    pe.matmul(attP[:, 0:P], GS[:, 0:P], WvT[:, :], start=True, stop=True)
                    pe.matmul(attP[:, P:2 * P], s_row[:, :], WvT[:, :], start=True, stop=True)
                    pe.matmul(attP[:, 2 * P:3 * P], s_row[:, :], ident[:, :],
                              start=True, stop=True).then_inc(att_pe, 1)
                if u == 20:
                    pe.wait_ge(att_seq, v + 9)
                    pe.matmul(attP[:, 0:P], WkT[:, :], P1[:, :], start=True, stop=True).then_inc(att_pe, 1)
                if u == 22:
                    pe.wait_ge(att_seq, v + 11)
                    pe.matmul(attP[:, 0:P + 1], Mm[:, :], Wq[:, :], start=True, stop=True)
                    pe.matmul(attP[:, 2 * P:3 * P], Wq[:, 0:P], Mm[:, :],
                              start=True, stop=True).then_inc(att_pe, 1)
                if u == 24:
                    pe.wait_ge(att_act, 6 * b + 5)
                    pe.matmul(attP[:, 0:P + 1], Am[:, :], Gc[:, :], start=True, stop=True).then_inc(att_pe, 1)
                if u == 26:
                    pe.wait_ge(att_seq, v + 13)
                    pe.matmul(attP[:, 2 * P:2 * P + 1], blkm[:, :], chmean[:, :],
                              start=True, stop=True).then_inc(att_pe, 1)
                if u == 27:
                    pe.wait_ge(att_seq, v + 15)
                    pe.matmul(attP[:, 3 * P:3 * P + 1], blkm[:, :], dev2[:, :],
                              start=True, stop=True).then_inc(att_pe, 1)
                if u == 29:
                    pe.wait_ge(att_seq, v + 20)
                    pe.matmul(attP[:, 0:P], ATs[:, :], WoT[:, :], start=True, stop=True)
                    pe.matmul(attP[:, P:2 * P], zb[:, :], WoT[:, :], start=True, stop=True).then_inc(att_pe, 1)
                if u in (31, 33):
                    g = (u - 31) // 2
                    if g == 0:
                        pe.wait_ge(att_act, 6 * b + 6)
                        pe.wait_ge(att_seq, v + 21)
                    else:
                        pe.wait_ge(attended, 2 * b + 1)
                    for j in range(TILES):
                        mm = pe.matmul(attP[:, j * P:(j + 1) * P], XAT[:, g * TILES + j, :], Bm[:, :],
                                       start=True, stop=True)
                    mm.then_inc(att_pe, 1)

            def pair(p, first, attention, last):
                n, t0 = PAIR * p, 2 * p
                for u in range(PAIR + (LAG if last else 0)):
                    w, s = u % UNITS, u // UNITS
                    if u < PAIR:
                        if first and u < UNITS:
                            pe.wait_ge(w_lo_done, u + 1)
                        if w == 0:
                            pe.wait_ge(xt_lo_ready, t0 + s + 1)
                        if not (first and u < 2):
                            pe.wait_ge(mul_done, n + u - 1)
                        for i, (dst, done) in enumerate(((gateP[u % 2], gate_done), (upP[u % 2], up_done))):
                            product(dst[:, :], W_hi[:, w, i, :], W_lo[:, w, i, :], XT_hi[:, s, :],
                                    XT_lo[:, s, :], True, True).then_inc(done, 1)
                    if not (first and u < LAG):
                        down(n, u - LAG, t0 + (u - LAG) // UNITS)
                    if w == 5 and not (first and s == 0):
                        transpose_back(t0 + s - 1)
                    if not (last and s >= 1):
                        if w == 4:
                            transpose_next(t0 + s + 1)
                        if w == 7:
                            logits(t0 + s + 1, (s + 1) % 2)
                        if w == 16:
                            transpose_weights(t0 + s + 1)
                    if attention:
                        attention_stage(u, p - ATT0)

            pe.wait_ge(const_seq, CONSTS)
            transpose_next(0)
            pe.wait_ge(small_in, 16 * 12)
            for i, w in enumerate((Wk_in, Wv_in, Wo_in)):
                pe.transpose(attP[:, i * P:(i + 1) * P], w[:, :], ident[:, :])
            pe.transpose(attP[:, 3 * P:3 * P + E], R_in[:, :], ident[0:E, 0:E]).then_inc(setup_psum, 1)
            pe.wait_ge(setup_sb, 5)
            logits(0, 0)
            transpose_weights(0)
            pair(0, True, False, False)
            with pe.Fori(ATT0, ATT1) as p:
                pair(p, False, True, False)
            with pe.Fori(ATT1, LAST) as p:
                pair(p, False, False, False)
            pair(LAST, False, False, True)
            transpose_back(STEPS - 1)

        @block.scalar
        def _(act):
            def split_high(unit):
                if unit == 0:
                    act.wait_ge(w_in[0], 48)
                if unit >= SHARED and (unit - SHARED) % ESEM == 0:
                    act.wait_ge(w_in[1 + (unit - SHARED) // ESEM], 48)
                act.copy(W_hi[:, unit, :, :], W_in[:, unit, :, :]).then_inc(w_hi_done, 1)

            def copy_y(t):
                act.wait_ge(down_done, UNITS * (t + 1))
                act.copy(YT[:, :], yP[:, :]).then_inc(y_copied, 1)

            def next_high(t, q):
                act.wait_ge(xt_done, t + 1)
                act.copy(XT_hi[:, q, :], prepP[:, :]).then_inc(xt_hi_ready, 1)

            def route_silu(t):
                act.wait_ge(route_seq, ROUTE_OPS * t + 3)
                act.activation(sil[:, :, :], lg[:, :, :], ACT.Silu).then_inc(silu_route, 1)

            def copy_weights(t):
                act.wait_ge(ct_done, t + 1)
                if not (isinstance(t, int) and t == 0):
                    act.wait_ge(ct_stored, 16 * t)
                act.copy(CT[:, :], prepP[0:E, :]).then_inc(ct_ready, 1)

            def attention_stage(u, b):
                if u in (13, 15):
                    g = (u - 13) // 2
                    act.wait_ge(att_pe, 12 * b + 1 + g)
                    act.copy(XAT[:, g * TILES:(g + 1) * TILES, :], attP[:, :]).then_inc(att_act, 1)
                if u == 17:
                    act.wait_ge(att_pe, 12 * b + 3)
                    act.copy(GS[:, :], attP[:, 0:P + 1]).then_inc(att_act, 1)
                if u == 23:
                    act.wait_ge(att_pe, 12 * b + 6)
                    act.copy(AT[:, :], attP[:, 0:P + 1]).then_inc(att_act, 1)
                    act.copy(Am[:, :], attP[:, 2 * P:3 * P]).then_inc(att_act, 1)
                if u == 30:
                    act.wait_ge(att_pe, 12 * b + 10)
                    act.copy(Bm[:, :], attP[:, 0:P]).then_inc(att_act, 1)

            def pair(p, first, attention, last):
                n, t0 = PAIR * p, 2 * p
                for u in range(PAIR + (LAG + 1 if last else 0)):
                    w, s = u % UNITS, u // UNITS
                    if w == LAG and not (first and s == 0):
                        copy_y(t0 + s - 1)
                    if u < PAIR:
                        act.wait_ge(gate_done, n + u + 1)
                        if not (first and u < 2):
                            act.wait_ge(mul_done, n + u - 1)
                        act.activation(S[:, u % 2, :], gateP[u % 2][:, :], ACT.Silu).then_inc(silu_done, 1)
                    if first and u + LAG < UNITS:
                        split_high(u + LAG)
                    if u <= PAIR and not (first and u == 0):
                        v = u - 1
                        if v % UNITS < SHARED:
                            act.wait_ge(mul_done, n + v + 1)
                        else:
                            act.wait_ge(weighted, E * t0 + v // UNITS * E + v % UNITS - SHARED + 1)
                        if not (first and v < 3):
                            act.wait_ge(down_done, n + v - 2)
                        act.copy(A_hi[:, v % 3, :], A[:, v % 3, :]).then_inc(high_done, 1)
                    if not (last and s >= 1):
                        if w == 5:
                            next_high(t0 + s + 1, (s + 1) % 2)
                        if w == 9:
                            route_silu(t0 + s + 1)
                        if w == 17:
                            copy_weights(t0 + s + 1)
                    if attention:
                        attention_stage(u, p - ATT0)

            next_high(0, 0)
            act.wait_ge(setup_psum, 1)
            act.copy(WkT[:, :], attP[:, 0:P]).then_inc(setup_sb, 1)
            act.copy(WvT[:, :], attP[:, P:2 * P]).then_inc(setup_sb, 1)
            act.copy(WoT[:, :], attP[:, 2 * P:3 * P]).then_inc(setup_sb, 1)
            act.copy(RT_hi[:, :], attP[:, 3 * P:3 * P + E]).then_inc(setup_sb, 1)
            for unit in range(LAG):
                split_high(unit)
            route_silu(0)
            copy_weights(0)
            pair(0, True, False, False)
            with act.Fori(ATT0, ATT1) as p:
                pair(p, False, True, False)
            with act.Fori(ATT1, LAST) as p:
                pair(p, False, False, False)
            pair(LAST, False, False, True)

        @block.vector
        def _(dve):
            def merge_stats(seq, base, halves, mean_out, var_out, tmp):
                dve.wait_ge(seq, base + 1)
                dve.tensor_tensor(tmp[:, 0, :], halves[:, :, 1], halves[:, :, 4], ALU.add)
                dve.tensor_tensor(tmp[:, 1, :], halves[:, :, 1], halves[:, :, 4], ALU.subtract)
                dve.tensor_tensor(tmp[:, 2, :], halves[:, :, 2], halves[:, :, 5], ALU.add).then_inc(seq, 1)
                dve.wait_ge(seq, base + 2)
                dve.tensor_scalar(mean_out, tmp[:, 0, :], 0.5, None, ALU.mult)
                dve.scalar_tensor_tensor(tmp[:, 3, :], tmp[:, 1, :], 0.25, tmp[:, 1, :], ALU.mult, ALU.mult)
                dve.tensor_scalar(tmp[:, 4, :], tmp[:, 2, :], 1.0 / P, EPS, ALU.mult,
                                  ALU.add).then_inc(seq, 1)
                dve.wait_ge(seq, base + 3)
                dve.tensor_tensor(var_out, tmp[:, 3, :], tmp[:, 4, :], ALU.add).then_inc(seq, 1)

            def stats(t, blk):
                for j in range(TILES):
                    ins = dve.bn_stats(bst[:, j, :], X[:, bass.ds(blk * TILES + j, 1), :]
                                       .rearrange("p o d -> p (o d)"))
                ins.then_inc(stats_seq, 1)
                merge_stats(stats_seq, 4 * t, bst, mean[:, :], vareps[:, :], parts)

            def normalise(t, blk):
                dve.wait_ge(rstd_ready, t + 1)
                for j in range(TILES):
                    ins = dve.tensor_scalar(XN[:, j, :], X[:, bass.ds(blk * TILES + j, 1), :]
                                            .rearrange("p o d -> p (o d)"),
                                            mean[:, j:j + 1], rstd[:, j:j + 1], ALU.subtract, ALU.mult)
                ins.then_inc(xn_ready, 1)

            def next_low(t, q):
                dve.wait_ge(xt_hi_ready, t + 1)
                dve.tensor_tensor(XT_lo[:, q, :], prepP[:, :], XT_hi[:, q, :].bitcast(F32),
                                  ALU.subtract).then_inc(xt_lo_ready, 1)

            G16 = TILES * GROUPS

            def route(t, part):
                base = ROUTE_OPS * t
                sel4 = sel[:, :, :].rearrange("p t (g i) -> p (t g) i", i=PER_GROUP)
                if part == 0:
                    dve.wait_ge(logits_done, t + 1)
                    flat = prepP[:, 0:TILES * E]
                    near_f = near[:, :, :].rearrange("p t e -> p (t e)")
                    dve.tensor_scalar(near_f, flat, -NEAR_ZERO, None, ALU.is_gt).then_inc(route_seq, 1)
                    dve.wait_ge(route_seq, base + 1)
                    dve.scalar_tensor_tensor(near_f, flat, NEAR_ZERO, near_f, ALU.is_lt,
                                             ALU.mult).then_inc(route_seq, 1)
                    dve.wait_ge(route_seq, base + 2)
                    dve.scalar_tensor_tensor(lg[:, :, :].rearrange("p t e -> p (t e)"), near_f, NEAR_ZERO,
                                             flat, ALU.mult, ALU.add).then_inc(route_seq, 1)
                    dve.wait_ge(route_seq, base + 3)
                    dve.reciprocal(rcl[:, :, :], lg[:, :, :]).then_inc(route_seq, 1)
                if part == 1:
                    dve.wait_ge(silu_route, t + 1)
                    dve.wait_ge(route_seq, base + 4)
                    dve.tensor_tensor(score[:, :, :], sil[:, :, :], rcl[:, :, :],
                                      ALU.mult).then_inc(route_seq, 1)
                    dve.wait_ge(route_seq, base + 5)
                    dve.tensor_tensor(sel[:, :, :], score[:, :, :], ebias[:, :, :],
                                      ALU.add).then_inc(route_seq, 1)
                    dve.wait_ge(route_seq, base + 6)
                    dve.tensor_tensor(hi2[:, :, :], sel4[:, :, 0:2], sel4[:, :, 2:4],
                                      ALU.max).then_inc(route_seq, 1)
                    dve.tensor_tensor(lo2[:, :, :], sel4[:, :, 0:2], sel4[:, :, 2:4],
                                      ALU.min).then_inc(route_seq, 1)
                if part == 2:
                    dve.wait_ge(route_seq, base + 8)
                    dve.tensor_tensor(top1[:, :], hi2[:, :, 0], hi2[:, :, 1], ALU.max).then_inc(route_seq, 1)
                    dve.tensor_tensor(mid[:, :], hi2[:, :, 0], hi2[:, :, 1], ALU.min).then_inc(route_seq, 1)
                    dve.tensor_tensor(low1[:, :], lo2[:, :, 0], lo2[:, :, 1], ALU.max).then_inc(route_seq, 1)
                    dve.wait_ge(route_seq, base + 11)
                    dve.tensor_tensor(mid[:, :], mid[:, :], low1[:, :], ALU.max).then_inc(route_seq, 1)
                    dve.wait_ge(route_seq, base + 12)
                    dve.tensor_tensor(gsc[:, :, :].rearrange("p t g -> p (t g)"), top1[:, :], mid[:, :],
                                      ALU.add).then_inc(route_seq, 1)
                if part == 3:
                    dve.wait_ge(route_seq, base + 13)
                    other = gsc[:, :, :].unsqueeze(2).broadcast_to([P, TILES, GROUPS, GROUPS])
                    own = gsc[:, :, :].unsqueeze(3).broadcast_to([P, TILES, GROUPS, GROUPS])
                    dve.tensor_tensor(gt[:, :, :, :], other, own, ALU.is_gt).then_inc(route_seq, 1)
                    dve.tensor_tensor(eq[:, :, :, :], other, own, ALU.is_equal).then_inc(route_seq, 1)
                    dve.wait_ge(route_seq, base + 15)
                    dve.tensor_tensor(eq[:, :, :, :], eq[:, :, :, :], before[:, :, :, :],
                                      ALU.mult).then_inc(route_seq, 1)
                    dve.wait_ge(route_seq, base + 16)
                    dve.tensor_tensor(gt[:, :, :, :], gt[:, :, :, :], eq[:, :, :, :],
                                      ALU.add).then_inc(route_seq, 1)
                    dve.wait_ge(route_seq, base + 17)
                    dve.tensor_reduce(grank[:, :], gt[:, :, :, :].rearrange("p t g h -> p (t g) h"),
                                      AX.X, ALU.add).then_inc(route_seq, 1)
                if part == 4:
                    dve.wait_ge(route_seq, base + 18)
                    dve.tensor_scalar(gmask[:, :], grank[:, :], float(TOP_GROUPS), None,
                                      ALU.is_lt).then_inc(route_seq, 1)
                    dve.wait_ge(route_seq, base + 19)
                    gm = gmask[:, :].unsqueeze(2).broadcast_to([P, G16, PER_GROUP])
                    pk = picked[:, :, :].rearrange("p t (g i) -> p (t g) i", i=PER_GROUP)
                    mk = masked[:, :, :].rearrange("p t (g i) -> p (t g) i", i=PER_GROUP)
                    dve.tensor_tensor(pk, sel4, gm, ALU.mult).then_inc(route_seq, 1)
                    dve.wait_ge(route_seq, base + 20)
                    dve.scalar_tensor_tensor(mk, gm, -1.0, pk, ALU.add, ALU.add).then_inc(route_seq, 1)
                if part == 5:
                    for j in range(TILES):
                        ins = dve.max(top8[:, j, :], masked[:, j, :])
                    ins.then_inc(route_seq, 1)
                if part == 6:
                    for j in range(TILES):
                        ins = dve.max_index(idx8[:, j, :], top8[:, j, :], masked[:, j, :])
                    ins.then_inc(route_seq, 1)
                    dve.wait_ge(route_seq, base + 23)
                    places = idx8[:, :, 0:TOP_K].unsqueeze(2).broadcast_to([P, TILES, E, TOP_K])
                    dve.tensor_tensor(hot[:, :, :, :], enum[:, :, :, :], places,
                                      ALU.is_equal).then_inc(route_seq, 1)
                if part == 7:
                    dve.wait_ge(route_seq, base + 24)
                    dve.tensor_reduce(emask[:, :, :], hot[:, :, :, :], AX.X, ALU.add).then_inc(route_seq, 1)
                    dve.wait_ge(route_seq, base + 25)
                    dve.tensor_tensor(wsel[:, :, :], emask[:, :, :], score[:, :, :],
                                      ALU.mult).then_inc(route_seq, 1)
                    dve.wait_ge(route_seq, base + 26)
                    dve.tensor_reduce(wsum[:, :], wsel[:, :, :], AX.X, ALU.add).then_inc(norm_seq, 1)
                    dve.wait_ge(norm_seq, 3 * t + 1)
                    dve.tensor_scalar(wsum[:, :], wsum[:, :], 1e-20, None, ALU.add).then_inc(norm_seq, 1)
                    dve.wait_ge(norm_seq, 3 * t + 2)
                    dve.reciprocal(wrec[:, :], wsum[:, :]).then_inc(norm_seq, 1)
                    dve.wait_ge(norm_seq, 3 * t + 3)
                    rec = wrec[:, :].unsqueeze(2).broadcast_to([P, TILES, E])
                    dve.scalar_tensor_tensor(comb[:, :, :], wsel[:, :, :], ROUTED_SCALE, rec,
                                             ALU.mult, ALU.mult).then_inc(route_seq, 1)

            def residual(t, blk):
                dve.wait_ge(y_back, t + 1)
                xb = X[:, bass.ds(blk * TILES, TILES), :].rearrange("p j d -> p (j d)")
                dve.scalar_tensor_tensor(xb, backP[:, :], 0.5, xb, ALU.mult,
                                         ALU.add).then_inc(x_updated, 1)

            def attention_stage(u, b):
                v = ATT_OPS * b
                if 6 < u <= 9 or u == 10:
                    j0 = 2 * (u - 7)
                    if u == 7:
                        dve.wait_ge(x_updated, 2 * b + 2)
                    for j in (j0, j0 + 1):
                        ins = dve.bn_stats(ast[:, j, :], X[:, bass.ds(b * BT + j, 1), :]
                                           .rearrange("p o d -> p (o d)"))
                    if u == 10:
                        ins.then_inc(att_seq, 1)
                        merge_stats(att_seq, v, ast, amean[:, :], avar[:, :], aparts)
                if u in (11, 12):
                    if u == 11:
                        dve.wait_ge(att_pow, 2 * b + 1)
                    for j in range(TILES * (u - 11), TILES * (u - 10)):
                        ins = dve.tensor_scalar(XA[:, j, 0:P], X[:, bass.ds(b * BT + j, 1), :]
                                                .rearrange("p o d -> p (o d)"),
                                                amean[:, j:j + 1], arstd[:, j:j + 1], ALU.subtract, ALU.mult)
                    if u == 12:
                        ins.then_inc(att_seq, 1)
                if u == 17:
                    dve.wait_ge(att_act, 6 * b + 3)
                    dve.tensor_scalar(s_row[:, :], ones[:, :], GS[:, P:P + 1], None,
                                      ALU.mult).then_inc(att_seq, 1)
                    dve.tensor_scalar(Gc[:, P:P + 1], GS[:, P:P + 1], 1.0 / SEQ, None, ALU.mult)
                    dve.tensor_scalar(nmu[:, :], GS[:, P:P + 1], -1.0 / SEQ / SEQ, None, ALU.mult)
                    dve.tensor_scalar(Gn[:, :], GS[:, 0:P], 1.0 / SEQ, None, ALU.mult).then_inc(att_seq, 1)
                if u == 19:
                    dve.wait_ge(att_pe, 12 * b + 4)
                    dve.wait_ge(att_seq, v + 7)
                    dve.scalar_tensor_tensor(P1[:, :], bvb[:, :], GS[:, P:P + 1], attP[:, 0:P],
                                             ALU.mult, ALU.add)
                    dve.scalar_tensor_tensor(rv[:, :], bvb[:, :], float(SEQ), attP[:, P:2 * P],
                                             ALU.mult, ALU.add).then_inc(att_seq, 1)
                    dve.scalar_tensor_tensor(Gc[:, 0:P], attP[:, 2 * P:3 * P], nmu[:, :], Gn[:, :],
                                             ALU.mult, ALU.add).then_inc(att_seq, 1)
                if u == 21:
                    dve.wait_ge(att_pe, 12 * b + 5)
                    dve.scalar_tensor_tensor(Mf[:, :], rv[:, :], bk[:, :], attP[:, 0:P],
                                             ALU.mult, ALU.add).then_inc(att_seq, 1)
                    dve.wait_ge(att_seq, v + 10)
                    dve.tensor_tensor(Mm[:, :], Mf[:, :], blk1[:, :], ALU.mult).then_inc(att_seq, 1)
                if u == 25:
                    dve.wait_ge(att_pe, 12 * b + 7)
                    dve.wait_ge(att_act, 6 * b + 5)
                    dve.tensor_tensor(quad[:, :], attP[:, 0:P], AT[:, 0:P], ALU.mult).then_inc(att_seq, 1)
                    dve.tensor_tensor(chmean[:, :], attP[:, P:P + 1], AT[:, P:P + 1],
                                      ALU.add).then_inc(att_seq, 1)
                if u == 26:
                    dve.wait_ge(att_seq, v + 13)
                    dve.tensor_reduce(chvar[:, :], quad[:, :], AX.X, ALU.add)
                    dve.wait_ge(att_pe, 12 * b + 8)
                    dve.tensor_copy(gmean[:, :], attP[:, 2 * P:2 * P + 1])
                    dve.tensor_tensor(dev[:, :], chmean[:, :], attP[:, 2 * P:2 * P + 1],
                                      ALU.subtract).then_inc(att_seq, 1)
                    dve.wait_ge(att_seq, v + 14)
                    dve.scalar_tensor_tensor(dev2[:, :], dev[:, :], dev[:, :], chvar[:, :],
                                             ALU.mult, ALU.add).then_inc(att_seq, 1)
                if u == 27:
                    dve.wait_ge(att_pe, 12 * b + 9)
                    dve.tensor_scalar(gvar[:, :], attP[:, 3 * P:3 * P + 1], EPS, None,
                                      ALU.add).then_inc(att_seq, 1)
                if u == 28:
                    dve.wait_ge(att_pow, 2 * b + 2)
                    dve.tensor_tensor(gsc1[:, :], grstd[:, :], gw[:, :], ALU.mult).then_inc(att_seq, 1)
                    dve.wait_ge(att_seq, v + 17)
                    dve.tensor_tensor(gms[:, :], gmean[:, :], gsc1[:, :], ALU.mult)
                    dve.tensor_scalar(ATs[:, :], AT[:, 0:P], gsc1[:, :], None, ALU.mult).then_inc(att_seq, 1)
                    dve.wait_ge(att_seq, v + 18)
                    dve.tensor_tensor(gsh[:, :], gb[:, :], gms[:, :], ALU.subtract).then_inc(att_seq, 1)
                    dve.wait_ge(att_seq, v + 19)
                    dve.scalar_tensor_tensor(z1[:, :], AT[:, P:P + 1], gsc1[:, :], gsh[:, :],
                                             ALU.mult, ALU.add).then_inc(z_ready, 1)
                    dve.wait_ge(z_ready, b + 1)
                    dve.tensor_scalar(zb[:, :], ones[:, :], z1[:, :], None, ALU.mult).then_inc(att_seq, 1)
                if u == 30:
                    dve.wait_ge(att_pe, 12 * b + 10)
                    dve.wait_ge(att_act, 6 * b + 6)
                    dve.tensor_tensor(brow[:, :], attP[:, P:2 * P], bob[:, :], ALU.add).then_inc(att_seq, 1)
                if u in (31, 33):
                    g = (u - 31) // 2
                    xb = X[:, bass.ds(b * BT + g * TILES, TILES), :]
                    dve.wait_ge(att_seq, v + 21)
                    dve.tensor_tensor(xb, xb, brow[:, :].unsqueeze(1).broadcast_to([P, TILES, P]),
                                      ALU.add).then_inc(row_added, 1)
                if u in (32, 34):
                    g = (u - 32) // 2
                    xb = X[:, bass.ds(b * BT + g * TILES, TILES), :].rearrange("p j d -> p (j d)")
                    dve.wait_ge(att_pe, 12 * b + 11 + g)
                    dve.wait_ge(row_added, 2 * b + 1 + g)
                    dve.tensor_tensor(xb, attP[:, :], xb, ALU.add).then_inc(attended, 1)

            def pair(p, first, attention, last):
                n, t0 = PAIR * p, 2 * p
                for u in range(PAIR):
                    w, s = u % UNITS, u // UNITS
                    if w in (13, 14) and not (last and s == 1):
                        dve.wait_ge(route_seq, ROUTE_OPS * (t0 + s + 1) + (21 if w == 13 else 22))
                    dve.wait_ge(silu_done, n + u + 1)
                    dve.wait_ge(up_done, n + u + 1)
                    if w < SHARED:
                        if not (first and u < 3):
                            dve.wait_ge(low_done, n + u - 2)
                        dve.tensor_tensor(A[:, u % 3, :], upP[u % 2][:, :], S[:, u % 2, :],
                                          ALU.mult).then_inc(mul_done, 1)
                    else:
                        e = w - SHARED
                        dve.tensor_tensor(SU[:, u % 2, :], upP[u % 2][:, :], S[:, u % 2, :],
                                          ALU.mult).then_inc(mul_done, 1)
                        dve.wait_ge(mul_done, n + u + 1)
                        if e % ESEM == 0:
                            dve.wait_ge(cb_in[e // ESEM], 16 * (t0 + s + 1))
                        if not (first and u < 3):
                            dve.wait_ge(low_done, n + u - 2)
                        dve.tensor_tensor(A[:, u % 3, :], SU[:, u % 2, :], CB[:, e, :],
                                          ALU.mult).then_inc(weighted, 1)
                    if w == 6 and not (first and s == 0):
                        residual(t0 + s - 1, 2 * mod(p - 1 + s, BATCH) + (1 - s))
                    if not (last and s == 1):
                        t, blk = t0 + s + 1, 2 * mod(p + s, BATCH) + (1 - s)
                        if w == 0:
                            if first and s == 0:
                                dve.wait_ge(x_rest, 16 * BATCH)
                            if not first:
                                dve.wait_ge(mul_done, n)
                            stats(t, blk)
                        if w == 2:
                            normalise(t, blk)
                        if w == 5:
                            next_low(t, (s + 1) % 2)
                        if 8 <= w < 16:
                            route(t, w - 8)
                    if attention:
                        attention_stage(u, p - ATT0)

            dve.wait_ge(x_first, 16)
            stats(0, 0)
            normalise(0, 0)
            next_low(0, 0)
            dve.wait_ge(const_seq, CONSTS)
            dve.tensor_scalar(blkm[:, :], blk1[:, :], 1.0 / HEAD, None, ALU.mult)
            dve.wait_ge(setup_sb, 4)
            dve.tensor_tensor(RT_lo[:, :], attP[:, 3 * P:3 * P + E], RT_hi[:, :].bitcast(F32),
                              ALU.subtract).then_inc(setup_sb, 1)
            dve.wait_ge(small_in, 16 * 12)
            for part in range(8):
                if part in (5, 6):
                    dve.wait_ge(route_seq, 21 if part == 5 else 22)
                route(0, part)
            pair(0, True, False, False)
            with dve.Fori(ATT0, ATT1) as p:
                pair(p, False, True, False)
            with dve.Fori(ATT1, LAST) as p:
                pair(p, False, False, False)
            pair(LAST, False, False, True)
            residual(STEPS - 1, NBLK - 1)


_INS = ["L0_attn_x", "L0_attn_Wqkv_w", "L0_attn_Wqkv_b", "L0_attn_gn_w", "L0_attn_gn_b",
        "L0_attn_out_w", "L0_attn_out_b", "L0_ffn_router_w", "L0_ffn_bias", "L0_ffn_gate_w",
        "L0_ffn_up_w", "L0_ffn_down_w", "L0_ffn_sh_gate_w", "L0_ffn_sh_up_w", "L0_ffn_sh_down_w"]
_OUTS = [((4, 1024, 128), "float32")]


def kernel(**inputs):
    import numpy as _np
    import concourse.bacc as _bacc
    from concourse import mybir as _mybir
    from concourse.bass_utils import run_bass_kernel_spmd as _run

    nc = _bacc.Bacc("TRN2", target_bir_lowering=False, num_devices=1)
    arrays, args = {}, []
    for name in _INS:
        a = _np.ascontiguousarray(inputs[name])
        arrays[f"in_{name}_dram"] = a
        args.append(nc.dram_tensor(f"in_{name}_dram", a.shape, _mybir.dt.from_np(a.dtype), kind="ExternalInput").ap())
    for i, (shape, dtype) in enumerate(_OUTS):
        dt = _mybir.dt.from_np(_np.dtype(dtype))
        args.append(nc.dram_tensor(f"out_{i}_dram", shape, dt, kind="ExternalOutput").ap())
    macaron_kernel(nc, *args)
    r = _run(nc, [arrays], core_ids=[0])
    got = tuple(r.results[0][f"out_{i}_dram"] for i in range(len(_OUTS)))
    return got[0]
```

```python
from contextlib import ExitStack

import concourse.bass as bass
from concourse import mybir

F32 = mybir.dt.float32
F32R = mybir.dt.float32r
U32 = mybir.dt.uint32
ALU = mybir.AluOpType
ACT = mybir.ActivationFunctionType
AX = mybir.AxisListType

P = 128
HEAD = 4
EPS = 1e-5
GROUPS, PER_GROUP = 4, 4
TOP_GROUPS, TOP_K = 2, 4
ROUTED_SCALE = 2.5
SHARED = 2
BLOCK = 512
TILES = BLOCK // P
NEAR_ZERO = 2.0 ** -24


def macaron_kernel(nc, x, Wqkv_w, Wqkv_b, gn_w, gn_b, out_w, out_b, router_w, bias,
                   gate_w, up_w, down_w, sh_gate_w, sh_up_w, sh_down_w, out):
    BATCH, SEQ, D = x.shape
    E = router_w.shape[0]
    UNITS = SHARED + E
    PAIR = 2 * UNITS
    BT = SEQ // P
    NBLK = BATCH * SEQ // BLOCK
    STEPS = 2 * NBLK
    PAIRS = STEPS // 2
    LAST = PAIRS - 1
    ATT0, ATT1 = 1, BATCH + 1
    LAG = 4
    SUS = 3
    SLOTS = 4
    POOL_WEIGHTED = (9, 11, 13, 15)
    ESEM = 4
    ROUTE_OPS = 27
    IDENT_AT = 4
    CONSTS = 12
    ATT_OPS = 20
    assert D == P and BT * P == SEQ and NBLK == 2 * BATCH and E == GROUPS * PER_GROUP

    x_v = x.rearrange("b (p j) d -> b p j d", j=BT)
    out_v = out.rearrange("b (p h j) d -> b h p j d", h=2, j=TILES)

    ctx = ExitStack()
    with ctx:
        def sb(name, shape, dt=F32):
            return ctx.enter_context(nc.sbuf_tensor(name, shape, dt))

        def pb(name):
            return ctx.enter_context(nc.psum_tensor(name, [P, 512], F32))

        def sem(name):
            return ctx.enter_context(nc.semaphore(name))

        X = sb("X", [P, BATCH * BT, P])
        W_in = sb("W_in", [P, UNITS, 3, P])
        W_hi = sb("W_hi", [P, UNITS, 3, P], F32R)
        W_lo = sb("W_lo", [P, UNITS, 3, P], F32R)
        XT_hi = sb("XT_hi", [P, 2, BLOCK], F32R)
        XT_lo = sb("XT_lo", [P, 2, BLOCK], F32R)
        S = sb("S", [P, 2, BLOCK])
        SU = sb("SU", [P, SUS, BLOCK])
        A = sb("A", [P, SLOTS, BLOCK])
        A_hi = sb("A_hi", [P, SLOTS, BLOCK], F32R)
        A_lo = sb("A_lo", [P, SLOTS, BLOCK], F32R)
        CB = sb("CB", [P, E, BLOCK])
        YT = sb("YT", [P, BLOCK])
        bst = sb("bst", [P, TILES, 6])
        parts = sb("parts", [P, 5, TILES])
        nmean = sb("nmean", [P, TILES])
        vareps = sb("vareps", [P, TILES])
        rstd = sb("rstd", [P, TILES])
        shift = sb("shift", [P, TILES])
        XN = sb("XN", [P, TILES, P])
        lg = sb("lg", [P, TILES, E])
        near = sb("near", [P, TILES, E])
        sil = sb("sil", [P, TILES, E])
        rcl = sb("rcl", [P, TILES, E])
        score = sb("score", [P, TILES, E])
        sel = sb("sel", [P, TILES, E])
        hi2 = sb("hi2", [P, TILES * GROUPS, 2])
        lo2 = sb("lo2", [P, TILES * GROUPS, 2])
        top1 = sb("top1", [P, TILES * GROUPS])
        mid = sb("mid", [P, TILES * GROUPS])
        low1 = sb("low1", [P, TILES * GROUPS])
        gsc = sb("gsc", [P, TILES, GROUPS])
        gt = sb("gt", [P, TILES, GROUPS, GROUPS])
        eq = sb("eq", [P, TILES, GROUPS, GROUPS])
        grank = sb("grank", [P, TILES * GROUPS])
        gmask = sb("gmask", [P, TILES * GROUPS])
        picked = sb("picked", [P, TILES, E])
        masked = sb("masked", [P, TILES, E])
        top8 = sb("top8", [P, TILES, 8])
        idx8 = sb("idx8", [P, TILES, 8], U32)
        hot = sb("hot", [P, TILES, E, TOP_K])
        emask = sb("emask", [P, TILES, E])
        wsel = sb("wsel", [P, TILES, E])
        wsum = sb("wsum", [P, TILES])
        wrec = sb("wrec", [P, TILES])
        comb = sb("comb", [P, TILES, E])
        CT = sb("CT", [E, BLOCK])
        ones = sb("ones", [P, P])
        ident = sb("ident", [P, P])
        half = sb("half", [P, BT])
        before = sb("before", [P, TILES, GROUPS, GROUPS])
        enum = sb("enum", [P, TILES, E, TOP_K])
        blk1 = sb("blk1", [P, P])
        blkm = sb("blkm", [P, P])
        R_in = sb("R_in", [E, P])
        RT_hi = sb("RT_hi", [P, E], F32R)
        RT_lo = sb("RT_lo", [P, E], F32R)
        ebias = sb("ebias", [P, TILES, E])
        Wq = sb("Wq", [P, P + 1])
        Wk_in = sb("Wk_in", [P, P])
        Wv_in = sb("Wv_in", [P, P])
        Wo_in = sb("Wo_in", [P, P])
        WkT = sb("WkT", [P, P])
        WvT = sb("WvT", [P, P])
        WoT = sb("WoT", [P, P])
        bk = sb("bk", [P, 1])
        bvb = sb("bvb", [P, P])
        bob = sb("bob", [P, P])
        gw = sb("gw", [P, 1])
        gb = sb("gb", [P, 1])
        ast = sb("ast", [P, BT, 6])
        aparts = sb("aparts", [P, 5, BT])
        anmean = sb("anmean", [P, BT])
        avar = sb("avar", [P, BT])
        arstd = sb("arstd", [P, BT])
        ashift = sb("ashift", [P, BT])
        XA = sb("XA", [P, BT, P + 1])
        XAT = sb("XAT", [P, BT, P])
        GS = sb("GS", [P, P + 1])
        s_row = sb("s_row", [P, P])
        nmu = sb("nmu", [P, 1])
        P1 = sb("P1", [P, P])
        rv = sb("rv", [P, P])
        Gn = sb("Gn", [P, P])
        Gc = sb("Gc", [P, P + 1])
        Mf = sb("Mf", [P, P])
        Mm = sb("Mm", [P, P])
        AT = sb("AT", [P, P + 1])
        Am = sb("Am", [P, P])
        quad = sb("quad", [P, P])
        chvar = sb("chvar", [P, 1])
        chmean = sb("chmean", [P, 1])
        dev = sb("dev", [P, 1])
        dev2 = sb("dev2", [P, 1])
        gvar = sb("gvar", [P, 1])
        gmean = sb("gmean", [P, 1])
        grstd = sb("grstd", [P, 1])
        gsc1 = sb("gsc1", [P, 1])
        gms = sb("gms", [P, 1])
        gsh = sb("gsh", [P, 1])
        z1 = sb("z1", [P, 1])
        zb = sb("zb", [P, P])
        ATs = sb("ATs", [P, P])
        Bm = sb("Bm", [P, P])
        brow = sb("brow", [P, P])

        gateP = [pb("gateP0"), pb("gateP1")]
        upP = [pb("upP0"), pb("upP1")]
        yP = pb("yP")
        prepP = pb("prepP")
        backP = pb("backP")
        attP = pb("attP")

        combT = nc.dram_tensor("combT", [STEPS, E, BLOCK], F32, kind="Internal").ap()

        x_first, x_rest = sem("x_first"), sem("x_rest")
        w_in = [sem(f"w_in{i}") for i in range(1 + E // ESEM)]
        router_in, small_in = sem("router_in"), sem("small_in")
        const_seq = sem("const_seq")
        w_hi_done, w_lo_done = sem("w_hi_done"), sem("w_lo_done")
        setup_psum, setup_sb = sem("setup_psum"), sem("setup_sb")
        gate_done, up_done, down_done = sem("gate_done"), sem("up_done"), sem("down_done")
        silu_done, mul_done = sem("silu_done"), sem("mul_done")
        weighted, pool_weighted = sem("weighted"), sem("pool_weighted")
        high_done, low_done = sem("high_done"), sem("low_done")
        y_copied, y_back, x_updated = sem("y_copied"), sem("y_back"), sem("x_updated")
        stats_seq, rstd_ready, xn_ready = sem("stats_seq"), sem("rstd_ready"), sem("xn_ready")
        xt_done, xt_hi_ready, xt_lo_ready = sem("xt_done"), sem("xt_hi_ready"), sem("xt_lo_ready")
        logits_done, silu_route, route_seq = sem("logits_done"), sem("silu_route"), sem("route_seq")
        norm_seq = sem("norm_seq")
        z_ready, row_added = sem("z_ready"), sem("row_added")
        ct_done, ct_ready, ct_stored = sem("ct_done"), sem("ct_ready"), sem("ct_stored")
        cb_in = [sem(f"cb_in{i}") for i in range(E // ESEM)]
        stored = sem("stored")
        att_seq = sem("att_seq")
        att_pow = sem("att_pow")
        att_pe = sem("att_pe")
        att_act = sem("att_act")
        xa_ready = sem("xa_ready")
        attended = sem("attended")

        block = ctx.enter_context(nc.Block())

        VE = E - len(POOL_WEIGHTED)
        POOLED = len(POOL_WEIGHTED)

        def weighted_by(step, w):
            if w in POOL_WEIGHTED:
                return pool_weighted, POOLED * step + POOL_WEIGHTED.index(w) + 1
            return weighted, VE * step + sum(v not in POOL_WEIGHTED for v in range(SHARED, w + 1))

        @block.sync
        def _(sp):
            sp.dma_start(X[:, 0:TILES, :], x_v[0][:, 0:TILES, :]).then_inc(x_first, 16)
            sp.dma_start(R_in[:, :], router_w).then_inc(router_in, 16)
            sp.dma_start(ebias[:, :, :], bias.unsqueeze(0).unsqueeze(0).broadcast_to([P, TILES, E])
                         ).then_inc(router_in, 16)
            for i, w in enumerate((sh_gate_w, sh_up_w)):
                sp.dma_start(W_in[:, 0:SHARED, i, :],
                             w.rearrange("d (s f) -> d s f", s=SHARED)).then_inc(w_in[0], 16)
            sp.dma_start(W_in[:, 0:SHARED, 2, :],
                         sh_down_w.rearrange("(s f) d -> f s d", s=SHARED)).then_inc(w_in[0], 16)
            for g in range(E // ESEM):
                for i, w in enumerate((gate_w, up_w, down_w)):
                    sp.dma_start(W_in[:, SHARED + g * ESEM:SHARED + (g + 1) * ESEM, i, :],
                                 w[g * ESEM:(g + 1) * ESEM].rearrange("e k m -> k e m")
                                 ).then_inc(w_in[1 + g], 16)
                if g == 0:
                    sp.dma_start(X[:, TILES:BT, :], x_v[0][:, TILES:BT, :]).then_inc(x_rest, 16)
            for b in range(1, BATCH):
                sp.dma_start(X[:, b * BT:(b + 1) * BT, :], x_v[b]).then_inc(x_rest, 16)

            def spread_weights(t, first):
                sp.wait_ge(ct_ready, t + 1)
                sp.dma_start(combT[bass.ds(t, 1)].rearrange("o e n -> (o e) n"),
                             CT[:, :]).then_inc(ct_stored, 16)
                sp.wait_ge(ct_stored, 16 * (t + 1))
                for g in range(E // ESEM):
                    if not first:
                        sp.wait_ge(high_done, UNITS * (t - 1) + SHARED + (g + 1) * ESEM)
                    src = combT[bass.ds(t, 1), g * ESEM:(g + 1) * ESEM, :]
                    sp.dma_start(CB[:, g * ESEM:(g + 1) * ESEM, :],
                                 src.broadcast_to([P, ESEM, BLOCK])).then_inc(cb_in[g], 16)

            def store(t):
                sp.wait_ge(x_updated, t + 1)
                blk = t - NBLK
                dst = out_v[bass.ds(blk // 2, 1), bass.ds(blk % 2, 1)]
                sp.dma_start(dst.rearrange("b h p j d -> (b h p) j d"),
                             X[:, bass.ds(blk * TILES, TILES), :]).then_inc(stored, 16)

            spread_weights(0, True)
            with sp.Fori(1, NBLK + 1) as t:
                spread_weights(t, False)
            with sp.Fori(NBLK + 1, STEPS) as t:
                spread_weights(t, False)
                store(t - 1)
            store(STEPS - 1)
            sp.wait_ge(stored, 16 * NBLK)

        @block.gpsimd
        def _(pool):
            def split_low(unit):
                pool.wait_ge(w_hi_done, unit + 1)
                pool.tensor_tensor(W_lo[:, unit, :, :], W_in[:, unit, :, :],
                                   W_hi[:, unit, :, :].bitcast(F32),
                                   ALU.subtract).then_inc(w_lo_done, 1)

            def split_activations(n, slot):
                pool.wait_ge(high_done, n + 1)
                pool.tensor_tensor(A_lo[:, slot, :], A[:, slot, :], A_hi[:, slot, :].bitcast(F32),
                                   ALU.subtract).then_inc(low_done, 1)

            def step_rstd(t):
                pool.wait_ge(stats_seq, 4 * (t + 1))
                pool.tensor_tensor(rstd[:, :], vareps[:, :], half[:, 0:TILES],
                                   ALU.pow).then_inc(rstd_ready, 1)
                pool.wait_ge(rstd_ready, 2 * t + 1)
                pool.tensor_tensor(shift[:, :], nmean[:, :], rstd[:, :], ALU.mult).then_inc(rstd_ready, 1)

            pool.memset(ident[:, :], 0.0).then_inc(const_seq, 1)
            pool.memset(half[:, :], -0.5).then_inc(const_seq, 1)
            pool.memset(ones[:, :], 1.0).then_inc(const_seq, 1)
            pool.wait_ge(const_seq, 3)
            pool.affine_select(out=ident[:, :], in_=ident[:, :], compare_op=ALU.not_equal, fill=1.0,
                               base=0, pattern=[[-1, P]], channel_multiplier=1).then_inc(const_seq, 1)
            step_rstd(0)
            pool.memset(before[:, :, :, :], 1.0).then_inc(const_seq, 1)
            pool.memset(XA[:, :, :], 1.0).then_inc(const_seq, 1)
            pool.memset(blk1[:, :], 1.0).then_inc(const_seq, 1)
            pool.memset(Gc[:, :], 0.0).then_inc(const_seq, 1)
            pool.iota(enum[:, :, :, :], pattern=[[0, TILES], [1, E], [0, TOP_K]], base=0,
                      channel_multiplier=0, allow_small_or_imprecise_dtypes=True).then_inc(const_seq, 1)
            pool.wait_ge(const_seq, 9)
            pool.affine_select(out=before[:, :, :, :], in_=before[:, :, :, :], compare_op=ALU.is_ge,
                               fill=0.0, base=-1, pattern=[[0, TILES], [1, GROUPS], [-1, GROUPS]],
                               channel_multiplier=0).then_inc(const_seq, 1)
            heads = blk1[:, :].rearrange("p (h c) -> p h c", c=HEAD)
            pool.affine_select(out=heads, in_=heads, compare_op=ALU.is_ge, fill=0.0, base=0,
                               pattern=[[-HEAD, P // HEAD], [0, HEAD]],
                               channel_multiplier=1).then_inc(const_seq, 1)
            pool.wait_ge(const_seq, 11)
            pool.affine_select(out=heads, in_=heads, compare_op=ALU.is_ge, fill=0.0, base=HEAD - 1,
                               pattern=[[HEAD, P // HEAD], [0, HEAD]],
                               channel_multiplier=-1).then_inc(const_seq, 1)

            def pair(p, first, attention, last):
                n = PAIR * p
                for u in range(PAIR):
                    w, s = u % UNITS, u // UNITS
                    if first and u + LAG < UNITS:
                        split_low(u + LAG)
                    if w in POOL_WEIGHTED:
                        pool.wait_ge(mul_done, n + u + 1)
                        pool.wait_ge(low_done, n + u + 1 - SLOTS)
                        pool.wait_ge(cb_in[(w - SHARED) // ESEM], 16 * (2 * p + s + 1))
                        pool.tensor_tensor(A[:, u % SLOTS, :], SU[:, u % SUS, :], CB[:, w - SHARED, :],
                                           ALU.mult).then_inc(pool_weighted, 1)
                    if w == 1 and not (last and s == 1):
                        step_rstd(2 * p + s + 1)
                    if attention and u == 10:
                        pool.wait_ge(att_seq, ATT_OPS * (p - ATT0) + 4)
                        pool.tensor_tensor(arstd[:, :], avar[:, :], half[:, :],
                                           ALU.pow).then_inc(att_pow, 1)
                        pool.wait_ge(att_pow, 3 * (p - ATT0) + 1)
                        pool.tensor_tensor(ashift[:, :], anmean[:, :], arstd[:, :],
                                           ALU.mult).then_inc(att_pow, 1)
                    if attention and u == 28:
                        pool.wait_ge(att_seq, ATT_OPS * (p - ATT0) + 15)
                        pool.tensor_tensor(grstd[:, :], gvar[:, :], half[:, 0:1],
                                           ALU.pow).then_inc(att_pow, 1)
                    if not (first and u == 0):
                        split_activations(n + u - 1, (u - 1) % SLOTS)

            for unit in range(LAG):
                split_low(unit)
            pair(0, True, False, False)
            with pool.Fori(ATT0, ATT1) as p:
                pair(p, False, True, False)
            with pool.Fori(ATT1, LAST) as p:
                pair(p, False, False, False)
            pair(LAST, False, False, True)
            split_activations(PAIR * PAIRS - 1, (PAIR - 1) % SLOTS)

        @block.tensor
        def _(pe):
            def product(dst, hi_w, lo_w, hi_x, lo_x, start, stop):
                pe.matmul(dst, hi_w, hi_x, start=start, stop=False)
                pe.matmul(dst, lo_w, hi_x, start=False, stop=False)
                return pe.matmul(dst, hi_w, lo_x, start=False, stop=stop)

            def down(n, u, t):
                w = u % UNITS
                if w == 0 and not (isinstance(t, int) and t == 0):
                    pe.wait_ge(y_copied, t)
                pe.wait_ge(low_done, n + u + 1)
                product(yP[:, :], W_hi[:, w, 2, :], W_lo[:, w, 2, :], A_hi[:, u % SLOTS, :],
                        A_lo[:, u % SLOTS, :], w == 0, w == UNITS - 1).then_inc(down_done, 1)

            def transpose_back(t):
                pe.wait_ge(y_copied, t + 1)
                for j in range(TILES):
                    mm = pe.transpose(backP[:, j * P:(j + 1) * P], YT[:, j * P:(j + 1) * P], ident[:, :])
                mm.then_inc(y_back, 1)

            def transpose_next(t):
                pe.wait_ge(xn_ready, t + 1)
                for j in range(TILES):
                    mm = pe.transpose(prepP[:, j * P:(j + 1) * P], XN[:, j, :], ident[:, :])
                mm.then_inc(xt_done, 1)

            def logits(t, q):
                pe.wait_ge(xt_lo_ready, t + 1)
                for j in range(TILES):
                    hi, lo = XT_hi[:, q, j * P:(j + 1) * P], XT_lo[:, q, j * P:(j + 1) * P]
                    mm = product(prepP[:, j * E:(j + 1) * E], hi, lo, RT_hi[:, :], RT_lo[:, :], True, True)
                mm.then_inc(logits_done, 1)

            def transpose_weights(t):
                pe.wait_ge(route_seq, ROUTE_OPS * (t + 1))
                for j in range(TILES):
                    mm = pe.transpose(prepP[0:E, j * P:(j + 1) * P], comb[:, j, :], ident[:, :])
                mm.then_inc(ct_done, 1)

            def attention_stage(u, b):
                v = ATT_OPS * b
                if u in (12, 14):
                    g = (u - 12) // 2
                    if g == 0:
                        pe.wait_ge(xa_ready, b + 1)
                    else:
                        pe.wait_ge(att_act, 6 * b + 1)
                    for j in range(TILES):
                        mm = pe.transpose(attP[:, j * P:(j + 1) * P], XA[:, g * TILES + j, 0:P], ident[:, :])
                    mm.then_inc(att_pe, 1)
                if u == 16:
                    pe.wait_ge(att_act, 6 * b + 2)
                    for j in range(BT):
                        mm = pe.matmul(attP[:, 0:P + 1], XA[:, j, 0:P], XA[:, j, :],
                                       start=(j == 0), stop=(j == BT - 1))
                    mm.then_inc(att_pe, 1)
                if u == 18:
                    pe.wait_ge(att_act, 6 * b + 3)
                    pe.wait_ge(att_seq, v + 5)
                    pe.matmul(attP[:, 0:P], GS[:, 0:P], WvT[:, :], start=True, stop=True)
                    pe.matmul(attP[:, P:2 * P], s_row[:, :], WvT[:, :], start=True, stop=True)
                    pe.matmul(attP[:, 2 * P:3 * P], s_row[:, :], ident[:, :],
                              start=True, stop=True).then_inc(att_pe, 1)
                if u == 20:
                    pe.wait_ge(att_seq, v + 8)
                    pe.matmul(attP[:, 0:P], WkT[:, :], P1[:, :], start=True, stop=True).then_inc(att_pe, 1)
                if u == 22:
                    pe.wait_ge(att_seq, v + 10)
                    pe.matmul(attP[:, 0:P + 1], Mm[:, :], Wq[:, :], start=True, stop=True)
                    pe.matmul(attP[:, 2 * P:3 * P], Wq[:, 0:P], Mm[:, :],
                              start=True, stop=True).then_inc(att_pe, 1)
                if u == 24:
                    pe.wait_ge(att_act, 6 * b + 5)
                    pe.matmul(attP[:, 0:P + 1], Am[:, :], Gc[:, :], start=True, stop=True).then_inc(att_pe, 1)
                if u == 26:
                    pe.wait_ge(att_seq, v + 12)
                    pe.matmul(attP[:, 2 * P:2 * P + 1], blkm[:, :], chmean[:, :],
                              start=True, stop=True).then_inc(att_pe, 1)
                if u == 27:
                    pe.wait_ge(att_seq, v + 14)
                    pe.matmul(attP[:, 3 * P:3 * P + 1], blkm[:, :], dev2[:, :],
                              start=True, stop=True).then_inc(att_pe, 1)
                if u == 29:
                    pe.wait_ge(att_seq, v + 19)
                    pe.matmul(attP[:, 0:P], ATs[:, :], WoT[:, :], start=True, stop=True)
                    pe.matmul(attP[:, P:2 * P], zb[:, :], WoT[:, :], start=True, stop=True).then_inc(att_pe, 1)
                if u in (31, 33):
                    g = (u - 31) // 2
                    if g == 0:
                        pe.wait_ge(att_act, 6 * b + 6)
                        pe.wait_ge(att_seq, v + 20)
                    else:
                        pe.wait_ge(attended, 2 * b + 1)
                    for j in range(TILES):
                        mm = pe.matmul(attP[:, j * P:(j + 1) * P], XAT[:, g * TILES + j, :], Bm[:, :],
                                       start=True, stop=True)
                    mm.then_inc(att_pe, 1)

            def pair(p, first, attention, last):
                n, t0 = PAIR * p, 2 * p
                for u in range(PAIR + (LAG if last else 0)):
                    w, s = u % UNITS, u // UNITS
                    if u < PAIR:
                        if first and u < UNITS:
                            pe.wait_ge(w_lo_done, u + 1)
                        if w == 0:
                            pe.wait_ge(xt_lo_ready, t0 + s + 1)
                        for i, (dst, done, left) in enumerate(((gateP[u % 2], gate_done, silu_done),
                                                               (upP[u % 2], up_done, mul_done))):
                            if not (first and u < 2):
                                pe.wait_ge(left, n + u - 1)
                            product(dst[:, :], W_hi[:, w, i, :], W_lo[:, w, i, :], XT_hi[:, s, :],
                                    XT_lo[:, s, :], True, True).then_inc(done, 1)
                    if not (first and u < LAG):
                        down(n, u - LAG, t0 + (u - LAG) // UNITS)
                    if w == 5 and not (first and s == 0):
                        transpose_back(t0 + s - 1)
                    if first and u == 2:
                        transpose_weights(0)
                    if not (last and s >= 1):
                        if w == 4:
                            transpose_next(t0 + s + 1)
                        if w == 7:
                            logits(t0 + s + 1, (s + 1) % 2)
                        if w == 16:
                            transpose_weights(t0 + s + 1)
                    if attention:
                        attention_stage(u, p - ATT0)

            pe.wait_ge(const_seq, IDENT_AT)
            pe.wait_ge(router_in, 32)
            pe.transpose(attP[:, 3 * P:3 * P + E], R_in[:, :], ident[0:E, 0:E]).then_inc(setup_psum, 1)
            transpose_next(0)
            pe.wait_ge(setup_sb, 2)
            logits(0, 0)
            pe.wait_ge(small_in, 16 * 10)
            for i, w in enumerate((Wk_in, Wv_in, Wo_in)):
                mm = pe.transpose(attP[:, i * P:(i + 1) * P], w[:, :], ident[:, :])
            mm.then_inc(setup_psum, 1)
            pair(0, True, False, False)
            with pe.Fori(ATT0, ATT1) as p:
                pair(p, False, True, False)
            with pe.Fori(ATT1, LAST) as p:
                pair(p, False, False, False)
            pair(LAST, False, False, True)
            transpose_back(STEPS - 1)

        @block.scalar
        def _(act):
            def split_high(unit):
                if unit == 0:
                    act.wait_ge(w_in[0], 48)
                if unit >= SHARED and (unit - SHARED) % ESEM == 0:
                    act.wait_ge(w_in[1 + (unit - SHARED) // ESEM], 48)
                act.copy(W_hi[:, unit, :, :], W_in[:, unit, :, :]).then_inc(w_hi_done, 1)

            def copy_y(t):
                act.wait_ge(down_done, UNITS * (t + 1))
                act.copy(YT[:, :], yP[:, :]).then_inc(y_copied, 1)

            def normalise(t, blk):
                act.wait_ge(rstd_ready, 2 * (t + 1))
                for j in range(TILES):
                    ins = act.activation(XN[:, j, :], X[:, bass.ds(blk * TILES + j, 1), :]
                                         .rearrange("p o d -> p (o d)"), ACT.Identity,
                                         scale=rstd[:, j:j + 1], bias=shift[:, j:j + 1])
                ins.then_inc(xn_ready, 1)

            def next_high(t, q):
                act.wait_ge(xt_done, t + 1)
                act.copy(XT_hi[:, q, :], prepP[:, :]).then_inc(xt_hi_ready, 1)

            def route_silu(t):
                act.wait_ge(route_seq, ROUTE_OPS * t + 3)
                act.activation(sil[:, :, :], lg[:, :, :], ACT.Silu).then_inc(silu_route, 1)

            def copy_weights(t):
                act.wait_ge(ct_done, t + 1)
                if not (isinstance(t, int) and t == 0):
                    act.wait_ge(ct_stored, 16 * t)
                act.copy(CT[:, :], prepP[0:E, :]).then_inc(ct_ready, 1)

            def attention_stage(u, b):
                if u in (11, 12):
                    if u == 11:
                        act.wait_ge(att_pow, 3 * b + 2)
                    for j in range(TILES * (u - 11), TILES * (u - 10)):
                        ins = act.activation(XA[:, j, 0:P], X[:, bass.ds(b * BT + j, 1), :]
                                             .rearrange("p o d -> p (o d)"), ACT.Identity,
                                             scale=arstd[:, j:j + 1], bias=ashift[:, j:j + 1])
                    if u == 12:
                        ins.then_inc(xa_ready, 1)
                if u in (13, 15):
                    g = (u - 13) // 2
                    act.wait_ge(att_pe, 12 * b + 1 + g)
                    act.copy(XAT[:, g * TILES:(g + 1) * TILES, :], attP[:, :]).then_inc(att_act, 1)
                if u == 17:
                    act.wait_ge(att_pe, 12 * b + 3)
                    act.copy(GS[:, :], attP[:, 0:P + 1]).then_inc(att_act, 1)
                if u == 23:
                    act.wait_ge(att_pe, 12 * b + 6)
                    act.copy(AT[:, :], attP[:, 0:P + 1]).then_inc(att_act, 1)
                    act.copy(Am[:, :], attP[:, 2 * P:3 * P]).then_inc(att_act, 1)
                if u == 30:
                    act.wait_ge(att_pe, 12 * b + 10)
                    act.copy(Bm[:, :], attP[:, 0:P]).then_inc(att_act, 1)

            def pair(p, first, attention, last):
                n, t0 = PAIR * p, 2 * p
                for u in range(PAIR + (LAG + 1 if last else 0)):
                    w, s = u % UNITS, u // UNITS
                    if w == LAG and not (first and s == 0):
                        copy_y(t0 + s - 1)
                    if u < PAIR:
                        act.wait_ge(gate_done, n + u + 1)
                        if not (first and u < 2):
                            act.wait_ge(mul_done, n + u - 1)
                        act.activation(S[:, u % 2, :], gateP[u % 2][:, :], ACT.Silu).then_inc(silu_done, 1)
                    if first and u + LAG < UNITS:
                        split_high(u + LAG)
                    if u <= PAIR and not (first and u == 0):
                        v = u - 1
                        if v % UNITS < SHARED:
                            act.wait_ge(mul_done, n + v + 1)
                        else:
                            act.wait_ge(*weighted_by(t0 + v // UNITS, v % UNITS))
                        if not (first and v < SLOTS):
                            act.wait_ge(down_done, n + v + 1 - SLOTS)
                        act.copy(A_hi[:, v % SLOTS, :], A[:, v % SLOTS, :]).then_inc(high_done, 1)
                    if first and u == 2:
                        copy_weights(0)
                    if not (last and s >= 1):
                        if w == 2:
                            normalise(t0 + s + 1, 2 * ((p + s) % BATCH) + (1 - s))
                        if w == 5:
                            next_high(t0 + s + 1, (s + 1) % 2)
                        if w == 9:
                            route_silu(t0 + s + 1)
                        if w == 17:
                            copy_weights(t0 + s + 1)
                    if attention:
                        attention_stage(u, p - ATT0)

            for dst, src in ((Wq[:, 0:P], Wqkv_w[0:P]),
                             (Wq[:, P:P + 1], Wqkv_b[0:P].unsqueeze(1)),
                             (Wk_in[:, :], Wqkv_w[P:2 * P]),
                             (Wv_in[:, :], Wqkv_w[2 * P:3 * P]),
                             (Wo_in[:, :], out_w),
                             (bk[:, :], Wqkv_b[P:2 * P].unsqueeze(1)),
                             (gw[:, :], gn_w.unsqueeze(1)),
                             (gb[:, :], gn_b.unsqueeze(1)),
                             (bvb[:, :], Wqkv_b[2 * P:3 * P].unsqueeze(0).broadcast_to([P, P])),
                             (bob[:, :], out_b.unsqueeze(0).broadcast_to([P, P]))):
                act.dma_start(dst, src).then_inc(small_in, 16)
            normalise(0, 0)
            next_high(0, 0)
            act.wait_ge(setup_psum, 1)
            act.copy(RT_hi[:, :], attP[:, 3 * P:3 * P + E]).then_inc(setup_sb, 1)
            for unit in range(SHARED):
                split_high(unit)
            act.wait_ge(setup_psum, 2)
            act.copy(WkT[:, :], attP[:, 0:P]).then_inc(setup_sb, 1)
            act.copy(WvT[:, :], attP[:, P:2 * P]).then_inc(setup_sb, 1)
            act.copy(WoT[:, :], attP[:, 2 * P:3 * P]).then_inc(setup_sb, 1)
            route_silu(0)
            for unit in range(SHARED, LAG):
                split_high(unit)
            pair(0, True, False, False)
            with act.Fori(ATT0, ATT1) as p:
                pair(p, False, True, False)
            with act.Fori(ATT1, LAST) as p:
                pair(p, False, False, False)
            pair(LAST, False, False, True)

        @block.vector
        def _(dve):
            def merge_stats(seq, base, halves, nmean_out, var_out, tmp):
                dve.wait_ge(seq, base + 1)
                dve.tensor_tensor(tmp[:, 0, :], halves[:, :, 1], halves[:, :, 4], ALU.add)
                dve.tensor_tensor(tmp[:, 1, :], halves[:, :, 1], halves[:, :, 4], ALU.subtract)
                dve.tensor_tensor(tmp[:, 2, :], halves[:, :, 2], halves[:, :, 5], ALU.add).then_inc(seq, 1)
                dve.wait_ge(seq, base + 2)
                dve.tensor_scalar(nmean_out, tmp[:, 0, :], -0.5, None, ALU.mult)
                dve.scalar_tensor_tensor(tmp[:, 3, :], tmp[:, 1, :], 0.25, tmp[:, 1, :], ALU.mult, ALU.mult)
                dve.tensor_scalar(tmp[:, 4, :], tmp[:, 2, :], 1.0 / P, EPS, ALU.mult,
                                  ALU.add).then_inc(seq, 1)
                dve.wait_ge(seq, base + 3)
                dve.tensor_tensor(var_out, tmp[:, 3, :], tmp[:, 4, :], ALU.add).then_inc(seq, 1)

            def stats(t, blk):
                for j in range(TILES):
                    ins = dve.bn_stats(bst[:, j, :], X[:, bass.ds(blk * TILES + j, 1), :]
                                       .rearrange("p o d -> p (o d)"))
                ins.then_inc(stats_seq, 1)
                merge_stats(stats_seq, 4 * t, bst, nmean[:, :], vareps[:, :], parts)

            def next_low(t, q):
                dve.wait_ge(xt_hi_ready, t + 1)
                dve.tensor_tensor(XT_lo[:, q, :], prepP[:, :], XT_hi[:, q, :].bitcast(F32),
                                  ALU.subtract).then_inc(xt_lo_ready, 1)

            G16 = TILES * GROUPS

            def route(t, part):
                base = ROUTE_OPS * t
                sel4 = sel[:, :, :].rearrange("p t (g i) -> p (t g) i", i=PER_GROUP)
                if part == 0:
                    dve.wait_ge(logits_done, t + 1)
                    flat = prepP[:, 0:TILES * E]
                    near_f = near[:, :, :].rearrange("p t e -> p (t e)")
                    dve.tensor_scalar(near_f, flat, -NEAR_ZERO, None, ALU.is_gt).then_inc(route_seq, 1)
                    dve.wait_ge(route_seq, base + 1)
                    dve.scalar_tensor_tensor(near_f, flat, NEAR_ZERO, near_f, ALU.is_lt,
                                             ALU.mult).then_inc(route_seq, 1)
                    dve.wait_ge(route_seq, base + 2)
                    dve.scalar_tensor_tensor(lg[:, :, :].rearrange("p t e -> p (t e)"), near_f, NEAR_ZERO,
                                             flat, ALU.mult, ALU.add).then_inc(route_seq, 1)
                    dve.wait_ge(route_seq, base + 3)
                    dve.reciprocal(rcl[:, :, :], lg[:, :, :]).then_inc(route_seq, 1)
                if part == 1:
                    dve.wait_ge(silu_route, t + 1)
                    dve.wait_ge(route_seq, base + 4)
                    dve.tensor_tensor(score[:, :, :], sil[:, :, :], rcl[:, :, :],
                                      ALU.mult).then_inc(route_seq, 1)
                    dve.wait_ge(route_seq, base + 5)
                    dve.tensor_tensor(sel[:, :, :], score[:, :, :], ebias[:, :, :],
                                      ALU.add).then_inc(route_seq, 1)
                    dve.wait_ge(route_seq, base + 6)
                    dve.tensor_tensor(hi2[:, :, :], sel4[:, :, 0:2], sel4[:, :, 2:4],
                                      ALU.max).then_inc(route_seq, 1)
                    dve.tensor_tensor(lo2[:, :, :], sel4[:, :, 0:2], sel4[:, :, 2:4],
                                      ALU.min).then_inc(route_seq, 1)
                if part == 2:
                    dve.wait_ge(route_seq, base + 8)
                    dve.tensor_tensor(top1[:, :], hi2[:, :, 0], hi2[:, :, 1], ALU.max).then_inc(route_seq, 1)
                    dve.tensor_tensor(mid[:, :], hi2[:, :, 0], hi2[:, :, 1], ALU.min).then_inc(route_seq, 1)
                    dve.tensor_tensor(low1[:, :], lo2[:, :, 0], lo2[:, :, 1], ALU.max).then_inc(route_seq, 1)
                    dve.wait_ge(route_seq, base + 11)
                    dve.tensor_tensor(mid[:, :], mid[:, :], low1[:, :], ALU.max).then_inc(route_seq, 1)
                    dve.wait_ge(route_seq, base + 12)
                    dve.tensor_tensor(gsc[:, :, :].rearrange("p t g -> p (t g)"), top1[:, :], mid[:, :],
                                      ALU.add).then_inc(route_seq, 1)
                if part == 3:
                    dve.wait_ge(route_seq, base + 13)
                    other = gsc[:, :, :].unsqueeze(2).broadcast_to([P, TILES, GROUPS, GROUPS])
                    own = gsc[:, :, :].unsqueeze(3).broadcast_to([P, TILES, GROUPS, GROUPS])
                    dve.tensor_tensor(gt[:, :, :, :], other, own, ALU.is_gt).then_inc(route_seq, 1)
                    dve.tensor_tensor(eq[:, :, :, :], other, own, ALU.is_equal).then_inc(route_seq, 1)
                    dve.wait_ge(route_seq, base + 15)
                    dve.tensor_tensor(eq[:, :, :, :], eq[:, :, :, :], before[:, :, :, :],
                                      ALU.mult).then_inc(route_seq, 1)
                    dve.wait_ge(route_seq, base + 16)
                    dve.tensor_tensor(gt[:, :, :, :], gt[:, :, :, :], eq[:, :, :, :],
                                      ALU.add).then_inc(route_seq, 1)
                    dve.wait_ge(route_seq, base + 17)
                    dve.tensor_reduce(grank[:, :], gt[:, :, :, :].rearrange("p t g h -> p (t g) h"),
                                      AX.X, ALU.add).then_inc(route_seq, 1)
                if part == 4:
                    dve.wait_ge(route_seq, base + 18)
                    dve.tensor_scalar(gmask[:, :], grank[:, :], float(TOP_GROUPS), None,
                                      ALU.is_lt).then_inc(route_seq, 1)
                    dve.wait_ge(route_seq, base + 19)
                    gm = gmask[:, :].unsqueeze(2).broadcast_to([P, G16, PER_GROUP])
                    pk = picked[:, :, :].rearrange("p t (g i) -> p (t g) i", i=PER_GROUP)
                    mk = masked[:, :, :].rearrange("p t (g i) -> p (t g) i", i=PER_GROUP)
                    dve.tensor_tensor(pk, sel4, gm, ALU.mult).then_inc(route_seq, 1)
                    dve.wait_ge(route_seq, base + 20)
                    dve.scalar_tensor_tensor(mk, gm, -1.0, pk, ALU.add, ALU.add).then_inc(route_seq, 1)
                if part == 5:
                    for j in range(TILES):
                        ins = dve.max(top8[:, j, :], masked[:, j, :])
                    ins.then_inc(route_seq, 1)
                if part == 6:
                    for j in range(TILES):
                        ins = dve.max_index(idx8[:, j, :], top8[:, j, :], masked[:, j, :])
                    ins.then_inc(route_seq, 1)
                    dve.wait_ge(route_seq, base + 23)
                    places = idx8[:, :, 0:TOP_K].unsqueeze(2).broadcast_to([P, TILES, E, TOP_K])
                    dve.tensor_tensor(hot[:, :, :, :], enum[:, :, :, :], places,
                                      ALU.is_equal).then_inc(route_seq, 1)
                if part == 7:
                    dve.wait_ge(route_seq, base + 24)
                    dve.tensor_reduce(emask[:, :, :], hot[:, :, :, :], AX.X, ALU.add).then_inc(route_seq, 1)
                    dve.wait_ge(route_seq, base + 25)
                    dve.tensor_tensor(wsel[:, :, :], emask[:, :, :], score[:, :, :],
                                      ALU.mult).then_inc(route_seq, 1)
                    dve.wait_ge(route_seq, base + 26)
                    dve.tensor_reduce(wsum[:, :], wsel[:, :, :], AX.X, ALU.add).then_inc(norm_seq, 1)
                    dve.wait_ge(norm_seq, 3 * t + 1)
                    dve.tensor_scalar(wsum[:, :], wsum[:, :], 1e-20, None, ALU.add).then_inc(norm_seq, 1)
                    dve.wait_ge(norm_seq, 3 * t + 2)
                    dve.reciprocal(wrec[:, :], wsum[:, :]).then_inc(norm_seq, 1)
                    dve.wait_ge(norm_seq, 3 * t + 3)
                    rec = wrec[:, :].unsqueeze(2).broadcast_to([P, TILES, E])
                    dve.scalar_tensor_tensor(comb[:, :, :], wsel[:, :, :], ROUTED_SCALE, rec,
                                             ALU.mult, ALU.mult).then_inc(route_seq, 1)

            def residual(t, blk):
                dve.wait_ge(y_back, t + 1)
                xb = X[:, bass.ds(blk * TILES, TILES), :].rearrange("p j d -> p (j d)")
                dve.scalar_tensor_tensor(xb, backP[:, :], 0.5, xb, ALU.mult,
                                         ALU.add).then_inc(x_updated, 1)

            def attention_stage(u, b):
                v = ATT_OPS * b
                if 6 < u <= 9 or u == 10:
                    j0 = 2 * (u - 7)
                    if u == 7:
                        dve.wait_ge(x_updated, 2 * b + 2)
                    for j in (j0, j0 + 1):
                        ins = dve.bn_stats(ast[:, j, :], X[:, bass.ds(b * BT + j, 1), :]
                                           .rearrange("p o d -> p (o d)"))
                    if u == 10:
                        ins.then_inc(att_seq, 1)
                        merge_stats(att_seq, v, ast, anmean[:, :], avar[:, :], aparts)
                if u == 17:
                    dve.wait_ge(att_act, 6 * b + 3)
                    dve.tensor_scalar(s_row[:, :], ones[:, :], GS[:, P:P + 1], None,
                                      ALU.mult).then_inc(att_seq, 1)
                    dve.tensor_scalar(Gc[:, P:P + 1], GS[:, P:P + 1], 1.0 / SEQ, None, ALU.mult)
                    dve.tensor_scalar(nmu[:, :], GS[:, P:P + 1], -1.0 / SEQ / SEQ, None, ALU.mult)
                    dve.tensor_scalar(Gn[:, :], GS[:, 0:P], 1.0 / SEQ, None, ALU.mult).then_inc(att_seq, 1)
                if u == 19:
                    dve.wait_ge(att_pe, 12 * b + 4)
                    dve.wait_ge(att_seq, v + 6)
                    dve.scalar_tensor_tensor(P1[:, :], bvb[:, :], GS[:, P:P + 1], attP[:, 0:P],
                                             ALU.mult, ALU.add)
                    dve.scalar_tensor_tensor(rv[:, :], bvb[:, :], float(SEQ), attP[:, P:2 * P],
                                             ALU.mult, ALU.add).then_inc(att_seq, 1)
                    dve.scalar_tensor_tensor(Gc[:, 0:P], attP[:, 2 * P:3 * P], nmu[:, :], Gn[:, :],
                                             ALU.mult, ALU.add).then_inc(att_seq, 1)
                if u == 21:
                    dve.wait_ge(att_pe, 12 * b + 5)
                    dve.scalar_tensor_tensor(Mf[:, :], rv[:, :], bk[:, :], attP[:, 0:P],
                                             ALU.mult, ALU.add).then_inc(att_seq, 1)
                    dve.wait_ge(att_seq, v + 9)
                    dve.tensor_tensor(Mm[:, :], Mf[:, :], blk1[:, :], ALU.mult).then_inc(att_seq, 1)
                if u == 25:
                    dve.wait_ge(att_pe, 12 * b + 7)
                    dve.wait_ge(att_act, 6 * b + 5)
                    dve.tensor_tensor(quad[:, :], attP[:, 0:P], AT[:, 0:P], ALU.mult).then_inc(att_seq, 1)
                    dve.tensor_tensor(chmean[:, :], attP[:, P:P + 1], AT[:, P:P + 1],
                                      ALU.add).then_inc(att_seq, 1)
                if u == 26:
                    dve.wait_ge(att_seq, v + 12)
                    dve.tensor_reduce(chvar[:, :], quad[:, :], AX.X, ALU.add)
                    dve.wait_ge(att_pe, 12 * b + 8)
                    dve.tensor_copy(gmean[:, :], attP[:, 2 * P:2 * P + 1])
                    dve.tensor_tensor(dev[:, :], chmean[:, :], attP[:, 2 * P:2 * P + 1],
                                      ALU.subtract).then_inc(att_seq, 1)
                    dve.wait_ge(att_seq, v + 13)
                    dve.scalar_tensor_tensor(dev2[:, :], dev[:, :], dev[:, :], chvar[:, :],
                                             ALU.mult, ALU.add).then_inc(att_seq, 1)
                if u == 27:
                    dve.wait_ge(att_pe, 12 * b + 9)
                    dve.tensor_scalar(gvar[:, :], attP[:, 3 * P:3 * P + 1], EPS, None,
                                      ALU.add).then_inc(att_seq, 1)
                if u == 28:
                    dve.wait_ge(att_pow, 3 * b + 3)
                    dve.tensor_tensor(gsc1[:, :], grstd[:, :], gw[:, :], ALU.mult).then_inc(att_seq, 1)
                    dve.wait_ge(att_seq, v + 16)
                    dve.tensor_tensor(gms[:, :], gmean[:, :], gsc1[:, :], ALU.mult)
                    dve.tensor_scalar(ATs[:, :], AT[:, 0:P], gsc1[:, :], None, ALU.mult).then_inc(att_seq, 1)
                    dve.wait_ge(att_seq, v + 17)
                    dve.tensor_tensor(gsh[:, :], gb[:, :], gms[:, :], ALU.subtract).then_inc(att_seq, 1)
                    dve.wait_ge(att_seq, v + 18)
                    dve.scalar_tensor_tensor(z1[:, :], AT[:, P:P + 1], gsc1[:, :], gsh[:, :],
                                             ALU.mult, ALU.add).then_inc(z_ready, 1)
                    dve.wait_ge(z_ready, b + 1)
                    dve.tensor_scalar(zb[:, :], ones[:, :], z1[:, :], None, ALU.mult).then_inc(att_seq, 1)
                if u == 30:
                    dve.wait_ge(att_pe, 12 * b + 10)
                    dve.wait_ge(att_act, 6 * b + 6)
                    dve.tensor_tensor(brow[:, :], attP[:, P:2 * P], bob[:, :], ALU.add).then_inc(att_seq, 1)
                if u in (31, 33):
                    g = (u - 31) // 2
                    xb = X[:, bass.ds(b * BT + g * TILES, TILES), :]
                    dve.wait_ge(att_seq, v + 20)
                    dve.tensor_tensor(xb, xb, brow[:, :].unsqueeze(1).broadcast_to([P, TILES, P]),
                                      ALU.add).then_inc(row_added, 1)
                if u in (32, 34):
                    g = (u - 32) // 2
                    xb = X[:, bass.ds(b * BT + g * TILES, TILES), :].rearrange("p j d -> p (j d)")
                    dve.wait_ge(att_pe, 12 * b + 11 + g)
                    dve.wait_ge(row_added, 2 * b + 1 + g)
                    dve.tensor_tensor(xb, attP[:, :], xb, ALU.add).then_inc(attended, 1)

            def weight(p, u, first):
                n, w, s = PAIR * p, u % UNITS, u // UNITS
                if w < SHARED or w in POOL_WEIGHTED:
                    return
                e = w - SHARED
                dve.wait_ge(mul_done, n + u + 1)
                if e % ESEM == 0 or w - 1 in POOL_WEIGHTED:
                    dve.wait_ge(cb_in[e // ESEM], 16 * (2 * p + s + 1))
                if not (first and u < SLOTS):
                    dve.wait_ge(low_done, n + u + 1 - SLOTS)
                dve.tensor_tensor(A[:, u % SLOTS, :], SU[:, u % SUS, :], CB[:, e, :],
                                  ALU.mult).then_inc(weighted, 1)

            def pair(p, first, attention, last):
                n, t0 = PAIR * p, 2 * p
                for u in range(PAIR):
                    w, s = u % UNITS, u // UNITS
                    if w in (13, 14) and not (last and s == 1):
                        dve.wait_ge(route_seq, ROUTE_OPS * (t0 + s + 1) + (21 if w == 13 else 22))
                    if not (first and u == 0):
                        weight(p, u - 1, first)
                    dve.wait_ge(silu_done, n + u + 1)
                    dve.wait_ge(up_done, n + u + 1)
                    if w < SHARED:
                        if not (first and u < SLOTS):
                            dve.wait_ge(low_done, n + u + 1 - SLOTS)
                        dst = A[:, u % SLOTS, :]
                    else:
                        if (w - SUS) in POOL_WEIGHTED:
                            dve.wait_ge(*weighted_by(t0 + s, w - SUS))
                        dst = SU[:, u % SUS, :]
                    dve.tensor_tensor(dst, upP[u % 2][:, :], S[:, u % 2, :], ALU.mult).then_inc(mul_done, 1)
                    if w == 6 and not (first and s == 0):
                        residual(t0 + s - 1, 2 * ((p - 1 + s) % BATCH) + (1 - s))
                    if not (last and s == 1):
                        t, blk = t0 + s + 1, 2 * ((p + s) % BATCH) + (1 - s)
                        if w == 0:
                            if first and s == 0:
                                dve.wait_ge(x_rest, 16 * BATCH)
                            if not first:
                                dve.wait_ge(mul_done, n)
                            stats(t, blk)
                        if w == 5:
                            next_low(t, (s + 1) % 2)
                        if 8 <= w < 16:
                            route(t, w - 8)
                    if attention:
                        attention_stage(u, p - ATT0)

            dve.wait_ge(x_first, 16)
            stats(0, 0)
            dve.wait_ge(setup_sb, 1)
            dve.tensor_tensor(RT_lo[:, :], attP[:, 3 * P:3 * P + E], RT_hi[:, :].bitcast(F32),
                              ALU.subtract).then_inc(setup_sb, 1)
            next_low(0, 0)
            dve.wait_ge(router_in, 32)
            dve.wait_ge(const_seq, CONSTS)
            dve.tensor_scalar(blkm[:, :], blk1[:, :], 1.0 / HEAD, None, ALU.mult)
            for part in range(8):
                if part in (5, 6):
                    dve.wait_ge(route_seq, 21 if part == 5 else 22)
                route(0, part)
            pair(0, True, False, False)
            with dve.Fori(ATT0, ATT1) as p:
                pair(p, False, True, False)
            with dve.Fori(ATT1, LAST) as p:
                pair(p, False, False, False)
            pair(LAST, False, False, True)
            weight(LAST, PAIR - 1, False)
            residual(STEPS - 1, NBLK - 1)


_INS = ["L0_attn_x", "L0_attn_Wqkv_w", "L0_attn_Wqkv_b", "L0_attn_gn_w", "L0_attn_gn_b",
        "L0_attn_out_w", "L0_attn_out_b", "L0_ffn_router_w", "L0_ffn_bias", "L0_ffn_gate_w",
        "L0_ffn_up_w", "L0_ffn_down_w", "L0_ffn_sh_gate_w", "L0_ffn_sh_up_w", "L0_ffn_sh_down_w"]
_OUTS = [((4, 1024, 128), "float32")]


def kernel(**inputs):
    import numpy as _np
    import concourse.bacc as _bacc
    from concourse import mybir as _mybir
    from concourse.bass_utils import run_bass_kernel_spmd as _run

    nc = _bacc.Bacc("TRN2", target_bir_lowering=False, num_devices=1)
    arrays, args = {}, []
    for name in _INS:
        a = _np.ascontiguousarray(inputs[name])
        arrays[f"in_{name}_dram"] = a
        args.append(nc.dram_tensor(f"in_{name}_dram", a.shape, _mybir.dt.from_np(a.dtype), kind="ExternalInput").ap())
    for i, (shape, dtype) in enumerate(_OUTS):
        dt = _mybir.dt.from_np(_np.dtype(dtype))
        args.append(nc.dram_tensor(f"out_{i}_dram", shape, dt, kind="ExternalOutput").ap())
    macaron_kernel(nc, *args)
    r = _run(nc, [arrays], core_ids=[0])
    got = tuple(r.results[0][f"out_{i}_dram"] for i in range(len(_OUTS)))
    return got[0]
```

```python
from contextlib import ExitStack

import concourse.bass as bass
from concourse import mybir

F32 = mybir.dt.float32
F32R = mybir.dt.float32r
U32 = mybir.dt.uint32
ALU = mybir.AluOpType
ACT = mybir.ActivationFunctionType
AX = mybir.AxisListType

P = 128
HEAD = 4
EPS = 1e-5
GROUPS, PER_GROUP = 4, 4
TOP_GROUPS, TOP_K = 2, 4
ROUTED_SCALE = 2.5
SHARED = 2
BLOCK = 512
TILES = BLOCK // P
NEAR_ZERO = 2.0 ** -24


def macaron_kernel(nc, x, Wqkv_w, Wqkv_b, gn_w, gn_b, out_w, out_b, router_w, bias,
                   gate_w, up_w, down_w, sh_gate_w, sh_up_w, sh_down_w, out):
    BATCH, SEQ, D = x.shape
    E = router_w.shape[0]
    UNITS = SHARED + E
    PAIR = 2 * UNITS
    BT = SEQ // P
    NBLK = BATCH * SEQ // BLOCK
    STEPS = 2 * NBLK
    PAIRS = STEPS // 2
    LAST = PAIRS - 1
    ATT0, ATT1 = 2, BATCH + 2
    LAG = 4
    SUS = 3
    SLOTS = 4
    POOL_WEIGHTED = (8, 10, 12, 14)
    ESEM = 4
    CSEM = 2
    AHEAD = 10
    ROUTE_OPS = 27
    CONSTS = 12
    IDENT_AT = 4
    ATT_OPS = 20
    assert D == P and BT * P == SEQ and NBLK == 2 * BATCH and E == GROUPS * PER_GROUP

    x_v = x.rearrange("b (p j) d -> b p j d", j=BT)
    out_v = out.rearrange("b (p h j) d -> b h p j d", h=2, j=TILES)

    ctx = ExitStack()
    with ctx:
        def sb(name, shape, dt=F32):
            return ctx.enter_context(nc.sbuf_tensor(name, shape, dt))

        def pb(name):
            return ctx.enter_context(nc.psum_tensor(name, [P, 512], F32))

        def sem(name):
            return ctx.enter_context(nc.semaphore(name))

        X = sb("X", [P, BATCH * BT, P])
        W_in = sb("W_in", [P, UNITS, 3, P])
        W_hi = sb("W_hi", [P, UNITS, 3, P], F32R)
        W_lo = sb("W_lo", [P, UNITS, 3, P], F32R)
        XT = sb("XT", [P, BLOCK])
        XT_hi = sb("XT_hi", [P, 2, BLOCK], F32R)
        XT_lo = sb("XT_lo", [P, 2, BLOCK], F32R)
        S = sb("S", [P, 2, BLOCK])
        SU = sb("SU", [P, SUS, BLOCK])
        A = sb("A", [P, SLOTS, BLOCK])
        A_hi = sb("A_hi", [P, SLOTS, BLOCK], F32R)
        A_lo = sb("A_lo", [P, SLOTS, BLOCK], F32R)
        CB = sb("CB", [P, E, BLOCK])
        YT = sb("YT", [P, BLOCK])
        bst = sb("bst", [P, TILES, 6])
        parts = sb("parts", [P, 5, TILES])
        nmean = sb("nmean", [P, TILES])
        vareps = sb("vareps", [P, TILES])
        rstd = sb("rstd", [P, TILES])
        shift = sb("shift", [P, TILES])
        XN = sb("XN", [P, TILES, P])
        lg = sb("lg", [P, TILES, E])
        near = sb("near", [P, TILES, E])
        sil = sb("sil", [P, TILES, E])
        rcl = sb("rcl", [P, TILES, E])
        score = sb("score", [P, TILES, E])
        sel = sb("sel", [P, TILES, E])
        hi2 = sb("hi2", [P, TILES * GROUPS, 2])
        lo2 = sb("lo2", [P, TILES * GROUPS, 2])
        top1 = sb("top1", [P, TILES * GROUPS])
        mid = sb("mid", [P, TILES * GROUPS])
        low1 = sb("low1", [P, TILES * GROUPS])
        gsc = sb("gsc", [P, TILES, GROUPS])
        gt = sb("gt", [P, TILES, GROUPS, GROUPS])
        eq = sb("eq", [P, TILES, GROUPS, GROUPS])
        grank = sb("grank", [P, TILES * GROUPS])
        gmask = sb("gmask", [P, TILES * GROUPS])
        picked = sb("picked", [P, TILES, E])
        masked = sb("masked", [P, TILES, E])
        top8 = sb("top8", [P, TILES, 8])
        idx8 = sb("idx8", [P, TILES, 8], U32)
        hot = sb("hot", [P, TILES, E, TOP_K])
        emask = sb("emask", [P, TILES, E])
        wsel = sb("wsel", [P, TILES, E])
        wsum = sb("wsum", [P, TILES])
        wrec = sb("wrec", [P, TILES])
        comb = sb("comb", [P, P])
        CT = sb("CT", [E * TILES, P])
        ones = sb("ones", [P, P])
        ident = sb("ident", [P, P])
        warm = sb("warm", [P, 1])
        half = sb("half", [P, BT])
        before = sb("before", [P, TILES, GROUPS, GROUPS])
        enum = sb("enum", [P, TILES, E, TOP_K])
        blk1 = sb("blk1", [P, P])
        blkm = sb("blkm", [P, P])
        R_in = sb("R_in", [E, P])
        RT = sb("RT", [P, E])
        ebias = sb("ebias", [P, TILES, E])
        Wq = sb("Wq", [P, P + 1])
        Wk_in = sb("Wk_in", [P, P])
        Wv_in = sb("Wv_in", [P, P])
        Wo_in = sb("Wo_in", [P, P])
        WkT = sb("WkT", [P, P])
        WvT = sb("WvT", [P, P])
        WoT = sb("WoT", [P, P])
        bk = sb("bk", [P, 1])
        bvb = sb("bvb", [P, P])
        bob = sb("bob", [P, P])
        gw = sb("gw", [P, 1])
        gb = sb("gb", [P, 1])
        ast = sb("ast", [P, BT, 6])
        aparts = sb("aparts", [P, 5, BT])
        anmean = sb("anmean", [P, BT])
        avar = sb("avar", [P, BT])
        arstd = sb("arstd", [P, BT])
        ashift = sb("ashift", [P, BT])
        XA = sb("XA", [P, BT, P + 1])
        XAT = sb("XAT", [P, BT, P])
        GS = sb("GS", [P, P + 1])
        s_row = sb("s_row", [P, P])
        nmu = sb("nmu", [P, 1])
        P1 = sb("P1", [P, P])
        rv = sb("rv", [P, P])
        Gn = sb("Gn", [P, P])
        Gc = sb("Gc", [P, P + 1])
        Mf = sb("Mf", [P, P])
        Mm = sb("Mm", [P, P])
        AT = sb("AT", [P, P + 1])
        Am = sb("Am", [P, P])
        quad = sb("quad", [P, P])
        chvar = sb("chvar", [P, 1])
        chmean = sb("chmean", [P, 1])
        dev = sb("dev", [P, 1])
        dev2 = sb("dev2", [P, 1])
        gvar = sb("gvar", [P, 1])
        gmean = sb("gmean", [P, 1])
        grstd = sb("grstd", [P, 1])
        gsc1 = sb("gsc1", [P, 1])
        gms = sb("gms", [P, 1])
        gsh = sb("gsh", [P, 1])
        z1 = sb("z1", [P, 1])
        zb = sb("zb", [P, P])
        ATs = sb("ATs", [P, P])
        Bm = P1
        brow = Mf

        gateP = [pb("gateP0"), pb("gateP1")]
        upP = [pb("upP0"), pb("upP1")]
        yP = pb("yP")
        prepP = pb("prepP")
        backP = pb("backP")
        attP = pb("attP")

        combT = nc.dram_tensor("combT", [STEPS, E, BLOCK], F32, kind="Internal").ap()

        x_first, x_rest = sem("x_first"), sem("x_rest")
        w_in = [sem(f"w_in{i}") for i in range(1 + E // ESEM)]
        router_in, small_in = sem("router_in"), sem("small_in")
        const_seq = sem("const_seq")
        w_hi_done, w_lo_done, w_lo_late = sem("w_hi_done"), sem("w_lo_done"), sem("w_lo_late")
        setup_psum, setup_sb = sem("setup_psum"), sem("setup_sb")
        gate_done, up_done, down_done = sem("gate_done"), sem("up_done"), sem("down_done")
        silu_done, mul_done = sem("silu_done"), sem("mul_done")
        weighted, pool_weighted = sem("weighted"), sem("pool_weighted")
        high_done, low_done = sem("high_done"), sem("low_done")
        y_copied, y_back, x_updated = sem("y_copied"), sem("y_back"), sem("x_updated")
        stats_seq, rstd_ready, xn_ready = sem("stats_seq"), sem("rstd_ready"), sem("xn_ready")
        xt_done, xt_hi_ready, xt_lo_ready = sem("xt_done"), sem("xt_hi_ready"), sem("xt_lo_ready")
        xt_ready = sem("xt_ready")
        logits_done, silu_route, route_seq = sem("logits_done"), sem("silu_route"), sem("route_seq")
        norm_seq = sem("norm_seq")
        z_ready, row_added = sem("z_ready"), sem("row_added")
        ct_done, ct_ready, ct_stored = sem("ct_done"), sem("ct_ready"), sem("ct_stored")
        cb_in = [sem(f"cb_in{i}") for i in range(E // CSEM)]
        stored = sem("stored")
        att_seq = sem("att_seq")
        att_pow = sem("att_pow")
        att_pe = sem("att_pe")
        att_act = sem("att_act")
        xa_ready = sem("xa_ready")
        attended = sem("attended")

        block = ctx.enter_context(nc.Block())

        VE = E - len(POOL_WEIGHTED)
        POOLED = len(POOL_WEIGHTED)

        def weighted_by(step, w):
            if w in POOL_WEIGHTED:
                return pool_weighted, POOLED * step + POOL_WEIGHTED.index(w) + 1
            return weighted, VE * step + sum(v not in POOL_WEIGHTED for v in range(SHARED, w + 1))

        @block.sync
        def _(sp):
            sp.dma_start(X[:, 0:TILES, :], x_v[0][:, 0:TILES, :]).then_inc(x_first, 16)
            sp.dma_start(R_in[:, :], router_w).then_inc(router_in, 16)
            sp.dma_start(ebias[:, :, :], bias.unsqueeze(0).unsqueeze(0).broadcast_to([P, TILES, E])
                         ).then_inc(router_in, 16)
            for i, w in enumerate((sh_gate_w, sh_up_w)):
                sp.dma_start(W_in[:, 0:SHARED, i, :],
                             w.rearrange("d (s f) -> d s f", s=SHARED)).then_inc(w_in[0], 16)
            sp.dma_start(W_in[:, 0:SHARED, 2, :],
                         sh_down_w.rearrange("(s f) d -> f s d", s=SHARED)).then_inc(w_in[0], 16)
            for g in range(E // ESEM):
                for i, w in enumerate((gate_w, up_w, down_w)):
                    sp.dma_start(W_in[:, SHARED + g * ESEM:SHARED + (g + 1) * ESEM, i, :],
                                 w[g * ESEM:(g + 1) * ESEM].rearrange("e k m -> k e m")
                                 ).then_inc(w_in[1 + g], 16)
                if g == 0:
                    sp.dma_start(X[:, TILES:BT, :], x_v[0][:, TILES:BT, :]).then_inc(x_rest, 16)
            for b in range(1, BATCH):
                sp.dma_start(X[:, b * BT:(b + 1) * BT, :], x_v[b]).then_inc(x_rest, 16)

            for dst, src in ((Wq[:, 0:P], Wqkv_w[0:P]),
                             (Wq[:, P:P + 1], Wqkv_b[0:P].unsqueeze(1)),
                             (Wk_in[:, :], Wqkv_w[P:2 * P]),
                             (Wv_in[:, :], Wqkv_w[2 * P:3 * P]),
                             (Wo_in[:, :], out_w),
                             (bk[:, :], Wqkv_b[P:2 * P].unsqueeze(1)),
                             (gw[:, :], gn_w.unsqueeze(1)),
                             (gb[:, :], gn_b.unsqueeze(1)),
                             (bvb[:, :], Wqkv_b[2 * P:3 * P].unsqueeze(0).broadcast_to([P, P])),
                             (bob[:, :], out_b.unsqueeze(0).broadcast_to([P, P]))):
                sp.dma_start(dst, src).then_inc(small_in, 16)

            def spread_weights(t, first):
                sp.wait_ge(ct_ready, t + 1)
                sp.dma_start(combT[bass.ds(t, 1)].rearrange("o e (j p) -> (o e j) p", p=P),
                             CT[:, :]).then_inc(ct_stored, 16)
                sp.wait_ge(ct_stored, 16 * (t + 1))
                for g in range(E // CSEM):
                    if not first:
                        sp.wait_ge(high_done, UNITS * (t - 1) + SHARED + (g + 1) * CSEM)
                    src = combT[bass.ds(t, 1), g * CSEM:(g + 1) * CSEM, :]
                    sp.dma_start(CB[:, g * CSEM:(g + 1) * CSEM, :],
                                 src.broadcast_to([P, CSEM, BLOCK])).then_inc(cb_in[g], 16)

            def store(t):
                sp.wait_ge(x_updated, t + 1)
                blk = t - NBLK
                dst = out_v[bass.ds(blk // 2, 1), bass.ds(blk % 2, 1)]
                sp.dma_start(dst.rearrange("b h p j d -> (b h p) j d"),
                             X[:, bass.ds(blk * TILES, TILES), :]).then_inc(stored, 16)

            spread_weights(0, True)
            with sp.Fori(1, NBLK + 1) as t:
                spread_weights(t, False)
            with sp.Fori(NBLK + 1, STEPS) as t:
                spread_weights(t, False)
                store(t - 1)
            store(STEPS - 1)
            sp.wait_ge(stored, 16 * NBLK)

        @block.gpsimd
        def _(pool):
            def split_low(unit):
                pool.wait_ge(w_hi_done, unit + 1)
                pool.tensor_tensor(W_lo[:, unit, :, :], W_in[:, unit, :, :],
                                   W_hi[:, unit, :, :].bitcast(F32),
                                   ALU.subtract).then_inc(w_lo_done, 1)

            def split_activations(n, slot):
                pool.wait_ge(high_done, n + 1)
                pool.tensor_tensor(A_lo[:, slot, :], A[:, slot, :], A_hi[:, slot, :].bitcast(F32),
                                   ALU.subtract).then_inc(low_done, 1)

            def step_rstd(t):
                pool.wait_ge(stats_seq, 4 * (t + 1))
                pool.tensor_tensor(rstd[:, :], vareps[:, :], half[:, 0:TILES],
                                   ALU.pow).then_inc(rstd_ready, 1)
                pool.wait_ge(rstd_ready, 2 * t + 1)
                pool.tensor_tensor(shift[:, :], nmean[:, :], rstd[:, :], ALU.mult).then_inc(rstd_ready, 1)

            def next_low(t, q):
                pool.wait_ge(xt_hi_ready, t + 1)
                pool.tensor_tensor(XT_lo[:, q, :], XT[:, :], XT_hi[:, q, :].bitcast(F32),
                                   ALU.subtract).then_inc(xt_lo_ready, 1)

            pool.memset(ident[:, :], 0.0).then_inc(const_seq, 1)
            pool.memset(half[:, :], -0.5).then_inc(const_seq, 1)
            pool.memset(ones[:, :], 1.0).then_inc(const_seq, 1)
            pool.wait_ge(const_seq, 3)
            pool.affine_select(out=ident[:, :], in_=ident[:, :], compare_op=ALU.not_equal, fill=1.0,
                               base=0, pattern=[[-1, P]], channel_multiplier=1).then_inc(const_seq, 1)
            step_rstd(0)
            pool.memset(before[:, :, :, :], 1.0).then_inc(const_seq, 1)
            pool.memset(XA[:, :, :], 1.0).then_inc(const_seq, 1)
            pool.memset(blk1[:, :], 1.0).then_inc(const_seq, 1)
            pool.memset(Gc[:, :], 0.0).then_inc(const_seq, 1)
            pool.iota(enum[:, :, :, :], pattern=[[0, TILES], [1, E], [0, TOP_K]], base=0,
                      channel_multiplier=0, allow_small_or_imprecise_dtypes=True).then_inc(const_seq, 1)
            pool.wait_ge(const_seq, 9)
            pool.affine_select(out=before[:, :, :, :], in_=before[:, :, :, :], compare_op=ALU.is_ge,
                               fill=0.0, base=-1, pattern=[[0, TILES], [1, GROUPS], [-1, GROUPS]],
                               channel_multiplier=0).then_inc(const_seq, 1)
            heads = blk1[:, :].rearrange("p (h c) -> p h c", c=HEAD)
            pool.affine_select(out=heads, in_=heads, compare_op=ALU.is_ge, fill=0.0, base=0,
                               pattern=[[-HEAD, P // HEAD], [0, HEAD]],
                               channel_multiplier=1).then_inc(const_seq, 1)
            pool.wait_ge(const_seq, 11)
            pool.affine_select(out=heads, in_=heads, compare_op=ALU.is_ge, fill=0.0, base=HEAD - 1,
                               pattern=[[HEAD, P // HEAD], [0, HEAD]],
                               channel_multiplier=-1).then_inc(const_seq, 1)

            def pair(p, first, attention, last):
                n = PAIR * p
                for u in range(PAIR):
                    w, s = u % UNITS, u // UNITS
                    if w in POOL_WEIGHTED:
                        pool.wait_ge(mul_done, n + u + 1)
                        pool.wait_ge(low_done, n + u + 1 - SLOTS)
                        pool.wait_ge(cb_in[(w - SHARED) // CSEM], 16 * (2 * p + s + 1))
                        pool.tensor_tensor(A[:, u % SLOTS, :], SU[:, u % SUS, :], CB[:, w - SHARED, :],
                                           ALU.mult).then_inc(pool_weighted, 1)
                    if w == 1 and not (last and s == 1):
                        step_rstd(2 * p + s + 1)
                    if w == 7 and not (last and s == 1):
                        next_low(2 * p + s + 1, (s + 1) % 2)
                    if attention and u == 5:
                        pool.wait_ge(att_seq, ATT_OPS * (p - ATT0) + 4)
                        pool.tensor_tensor(arstd[:, :], avar[:, :], half[:, :],
                                           ALU.pow).then_inc(att_pow, 1)
                        pool.wait_ge(att_pow, 3 * (p - ATT0) + 1)
                        pool.tensor_tensor(ashift[:, :], anmean[:, :], arstd[:, :],
                                           ALU.mult).then_inc(att_pow, 1)
                    if attention and u == 30:
                        pool.wait_ge(att_seq, ATT_OPS * (p - ATT0) + 15)
                        pool.tensor_tensor(grstd[:, :], gvar[:, :], half[:, 0:1],
                                           ALU.pow).then_inc(att_pow, 1)
                    if not (first and u == 0):
                        split_activations(n + u - 1, (u - 1) % SLOTS)

            for unit in range(AHEAD):
                split_low(unit)
            pair(0, True, False, False)
            for p in range(1, ATT0):
                pair(p, False, False, False)
            with pool.Fori(ATT0, ATT1) as p:
                pair(p, False, True, False)
            for p in range(ATT1, LAST):
                pair(p, False, False, False)
            pair(LAST, False, False, True)
            split_activations(PAIR * PAIRS - 1, (PAIR - 1) % SLOTS)

        @block.tensor
        def _(pe):
            def product(dst, hi_w, lo_w, hi_x, lo_x, start, stop):
                pe.matmul(dst, hi_w, hi_x, start=start, stop=False)
                pe.matmul(dst, lo_w, hi_x, start=False, stop=False)
                return pe.matmul(dst, hi_w, lo_x, start=False, stop=stop)

            def down(n, u, t):
                w = u % UNITS
                if w == 0 and not (isinstance(t, int) and t == 0):
                    pe.wait_ge(y_copied, t)
                pe.wait_ge(low_done, n + u + 1)
                product(yP[:, :], W_hi[:, w, 2, :], W_lo[:, w, 2, :], A_hi[:, u % SLOTS, :],
                        A_lo[:, u % SLOTS, :], w == 0, w == UNITS - 1).then_inc(down_done, 1)

            def transpose_back(t):
                pe.wait_ge(y_copied, t + 1)
                for j in range(TILES):
                    mm = pe.transpose(backP[:, j * P:(j + 1) * P], YT[:, j * P:(j + 1) * P], ident[:, :])
                mm.then_inc(y_back, 1)

            def transpose_next(t):
                pe.wait_ge(xn_ready, 2 * (t + 1))
                for j in range(TILES):
                    mm = pe.transpose(prepP[:, j * P:(j + 1) * P], XN[:, j, :], ident[:, :])
                mm.then_inc(xt_done, 1)

            def logits(t):
                pe.wait_ge(xt_ready, t + 1)
                for j in range(TILES):
                    mm = pe.matmul(prepP[:, j * E:(j + 1) * E], XT[:, j * P:(j + 1) * P], RT[:, :],
                                   start=True, stop=True)
                mm.then_inc(logits_done, 1)

            def transpose_weights(t):
                pe.wait_ge(route_seq, ROUTE_OPS * (t + 1))
                pe.transpose(prepP[:, 0:P], comb[:, :], ident[:, :]).then_inc(ct_done, 1)

            def attention_stage(u, b):
                v = ATT_OPS * b
                if u == 12:
                    pe.wait_ge(xa_ready, b + 1)
                    for j in range(BT):
                        mm = pe.matmul(attP[:, 0:P + 1], XA[:, j, 0:P], XA[:, j, :],
                                       start=(j == 0), stop=(j == BT - 1))
                    mm.then_inc(att_pe, 1)
                if u in (12, 15):
                    g = (u - 12) // 3
                    if g == 0:
                        pe.wait_ge(x_updated, 2 * (b + ATT0))
                    else:
                        pe.wait_ge(att_act, 6 * b + 2)
                    for j in range(TILES):
                        mm = pe.transpose(backP[:, j * P:(j + 1) * P], XA[:, g * TILES + j, 0:P], ident[:, :])
                    mm.then_inc(att_pe, 1)
                if u == 16:
                    pe.wait_ge(att_act, 6 * b + 1)
                    pe.wait_ge(att_seq, v + 5)
                    pe.matmul(attP[:, 0:P], GS[:, 0:P], WvT[:, :], start=True, stop=True)
                    pe.matmul(attP[:, P:2 * P], s_row[:, :], WvT[:, :], start=True, stop=True)
                    pe.matmul(attP[:, 2 * P:3 * P], s_row[:, :], ident[:, :],
                              start=True, stop=True).then_inc(att_pe, 1)
                if u == 19:
                    pe.wait_ge(att_seq, v + 8)
                    pe.matmul(attP[:, 0:P], WkT[:, :], P1[:, :], start=True, stop=True).then_inc(att_pe, 1)
                if u == 21:
                    pe.wait_ge(att_seq, v + 10)
                    pe.matmul(attP[:, 0:P + 1], Mm[:, :], Wq[:, :], start=True, stop=True)
                    pe.matmul(attP[:, 2 * P:3 * P], Wq[:, 0:P], Mm[:, :],
                              start=True, stop=True).then_inc(att_pe, 1)
                if u == 23:
                    pe.wait_ge(att_act, 6 * b + 5)
                    pe.matmul(attP[:, 0:P + 1], Am[:, :], Gc[:, :], start=True, stop=True).then_inc(att_pe, 1)
                if u == 26:
                    pe.wait_ge(att_seq, v + 12)
                    pe.matmul(attP[:, 2 * P:2 * P + 1], blkm[:, :], chmean[:, :],
                              start=True, stop=True).then_inc(att_pe, 1)
                if u == 29:
                    pe.wait_ge(att_seq, v + 14)
                    pe.matmul(attP[:, 3 * P:3 * P + 1], blkm[:, :], dev2[:, :],
                              start=True, stop=True).then_inc(att_pe, 1)
                if u == 32:
                    pe.wait_ge(att_seq, v + 19)
                    pe.matmul(attP[:, 0:P], ATs[:, :], WoT[:, :], start=True, stop=True)
                    pe.matmul(attP[:, P:2 * P], zb[:, :], WoT[:, :], start=True, stop=True).then_inc(att_pe, 1)
                if u == 34:
                    pe.wait_ge(att_act, 6 * b + 6)
                    pe.wait_ge(att_seq, v + 20)
                    pe.wait_ge(x_updated, 2 * (b + ATT0) + 1)
                    for g, bank in enumerate((attP, backP)):
                        for j in range(TILES):
                            mm = pe.matmul(bank[:, j * P:(j + 1) * P], XAT[:, g * TILES + j, :], Bm[:, :],
                                           start=True, stop=True)
                        mm.then_inc(att_pe, 1)

            def pair(p, first, attention, last, after=False):
                n, t0 = PAIR * p, 2 * p
                for u in range(PAIR + (LAG if last else 0)):
                    w, s = u % UNITS, u // UNITS
                    if u < PAIR:
                        if first and u < UNITS:
                            if u < AHEAD:
                                pe.wait_ge(w_lo_done, u + 1)
                            else:
                                pe.wait_ge(w_lo_late, u + 1 - AHEAD)
                        if w == 0:
                            pe.wait_ge(xt_lo_ready, t0 + s + 1)
                        for i, (dst, done, left) in enumerate(((gateP[u % 2], gate_done, silu_done),
                                                               (upP[u % 2], up_done, mul_done))):
                            if not (first and u < 2):
                                pe.wait_ge(left, n + u - 1)
                            product(dst[:, :], W_hi[:, w, i, :], W_lo[:, w, i, :], XT_hi[:, s, :],
                                    XT_lo[:, s, :], True, True).then_inc(done, 1)
                    if not (first and u < LAG):
                        down(n, u - LAG, t0 + (u - LAG) // UNITS)
                    if w == 6 and not (first and s == 0):
                        if attention and s == 1:
                            pe.wait_ge(att_act, 6 * (p - ATT0) + 3)
                        if s == 0 and after:
                            pe.wait_ge(attended, 2 * (p - ATT0 + 1))
                        transpose_back(t0 + s - 1)
                    if first and u == 1:
                        transpose_weights(0)
                    if first and u == 6:
                        pe.wait_ge(small_in, 16 * 10)
                        for i, matrix in enumerate((Wk_in, Wv_in, Wo_in)):
                            mm = pe.transpose(attP[:, i * P:(i + 1) * P], matrix[:, :], ident[:, :])
                        mm.then_inc(setup_psum, 1)
                    if not (last and s >= 1):
                        if w == 5:
                            transpose_next(t0 + s + 1)
                        if w == 7:
                            logits(t0 + s + 1)
                        if w == 16:
                            transpose_weights(t0 + s + 1)
                    if attention:
                        attention_stage(u, p - ATT0)

            pe.wait_ge(const_seq, IDENT_AT)
            pe.wait_ge(router_in, 32)
            pe.transpose(attP[:, 3 * P:3 * P + E], R_in[:, :], ident[0:E, 0:E]).then_inc(setup_psum, 1)
            transpose_next(0)
            pe.wait_ge(setup_sb, 1)
            logits(0)
            pair(0, True, False, False)
            for p in range(1, ATT0):
                pair(p, False, False, False)
            with pe.Fori(ATT0, ATT1) as p:
                pair(p, False, True, False, True)
            for p in range(ATT1, LAST):
                pair(p, False, False, False, p == ATT1)
            pair(LAST, False, False, True)
            transpose_back(STEPS - 1)

        @block.scalar
        def _(act):
            def split_high(unit):
                if unit == 0:
                    act.wait_ge(w_in[0], 48)
                if unit >= SHARED and (unit - SHARED) % ESEM == 0:
                    act.wait_ge(w_in[1 + (unit - SHARED) // ESEM], 48)
                act.copy(W_hi[:, unit, :, :], W_in[:, unit, :, :]).then_inc(w_hi_done, 1)

            def copy_y(t):
                act.wait_ge(down_done, UNITS * (t + 1))
                act.copy(YT[:, :], yP[:, :]).then_inc(y_copied, 1)

            def normalise(t, blk, part):
                act.wait_ge(rstd_ready, 2 * (t + 1))
                for j in range(part * TILES // 2, (part + 1) * TILES // 2):
                    ins = act.activation(XN[:, j, :], X[:, bass.ds(blk * TILES + j, 1), :]
                                         .rearrange("p o d -> p (o d)"), ACT.Identity,
                                         scale=rstd[:, j:j + 1], bias=shift[:, j:j + 1])
                ins.then_inc(xn_ready, 1)

            def next_high(t, q):
                act.wait_ge(xt_ready, t + 1)
                act.copy(XT_hi[:, q, :], XT[:, :]).then_inc(xt_hi_ready, 1)

            def route_silu(t):
                act.wait_ge(route_seq, ROUTE_OPS * t + 3)
                act.activation(sil[:, :, :], lg[:, :, :], ACT.Silu).then_inc(silu_route, 1)

            def copy_weights(t):
                act.wait_ge(ct_done, t + 1)
                if not (isinstance(t, int) and t == 0):
                    act.wait_ge(ct_stored, 16 * t)
                act.copy(CT[:, :], prepP[0:E * TILES, 0:P]).then_inc(ct_ready, 1)

            def attention_stage(u, b):
                if 7 <= u < 11:
                    if u == 7:
                        act.wait_ge(att_pow, 3 * b + 2)
                    for j in range(2 * (u - 7), 2 * (u - 6)):
                        ins = act.activation(XA[:, j, 0:P], X[:, bass.ds(b * BT + j, 1), :]
                                             .rearrange("p o d -> p (o d)"), ACT.Identity,
                                             scale=arstd[:, j:j + 1], bias=ashift[:, j:j + 1])
                    if u == 10:
                        ins.then_inc(xa_ready, 1)
                if u == 13:
                    act.wait_ge(att_pe, 12 * b + 1)
                    act.copy(GS[:, :], attP[:, 0:P + 1]).then_inc(att_act, 1)
                if u in (13, 16):
                    g = (u - 13) // 3
                    act.wait_ge(att_pe, 12 * b + 2 + g)
                    act.copy(XAT[:, g * TILES:(g + 1) * TILES, :], backP[:, :]).then_inc(att_act, 1)
                if u == 22:
                    act.wait_ge(att_pe, 12 * b + 6)
                    act.copy(AT[:, :], attP[:, 0:P + 1]).then_inc(att_act, 1)
                    act.copy(Am[:, :], attP[:, 2 * P:3 * P]).then_inc(att_act, 1)
                if u == 33:
                    act.wait_ge(att_pe, 12 * b + 10)
                    act.copy(Bm[:, :], attP[:, 0:P]).then_inc(att_act, 1)

            def pair(p, first, attention, last):
                n, t0 = PAIR * p, 2 * p
                for u in range(PAIR + (LAG + 1 if last else 0)):
                    w, s = u % UNITS, u // UNITS
                    if w == LAG and not (first and s == 0):
                        copy_y(t0 + s - 1)
                    if u < PAIR:
                        act.wait_ge(gate_done, n + u + 1)
                        if not (first and u < 2):
                            act.wait_ge(mul_done, n + u - 1)
                        act.activation(S[:, u % 2, :], gateP[u % 2][:, :], ACT.Silu).then_inc(silu_done, 1)
                    if first and u == 1:
                        copy_weights(0)
                    if first and u == 7:
                        act.wait_ge(setup_psum, 2)
                        for i, matrix in enumerate((WkT, WvT, WoT)):
                            act.copy(matrix[:, :], attP[:, i * P:(i + 1) * P]).then_inc(setup_sb, 1)
                    if first and u + AHEAD < UNITS:
                        split_high(u + AHEAD)
                    if u <= PAIR and not (first and u == 0):
                        v = u - 1
                        if v % UNITS < SHARED:
                            act.wait_ge(mul_done, n + v + 1)
                        else:
                            act.wait_ge(*weighted_by(t0 + v // UNITS, v % UNITS))
                        if not (first and v < SLOTS):
                            act.wait_ge(down_done, n + v + 1 - SLOTS)
                        act.copy(A_hi[:, v % SLOTS, :], A[:, v % SLOTS, :]).then_inc(high_done, 1)
                    if not (last and s >= 1):
                        if w in (2, 3 if first and s == 0 else 4):
                            normalise(t0 + s + 1, 2 * ((p + s) % BATCH) + (1 - s), (w - 1) // 2)
                        if w == 6:
                            next_high(t0 + s + 1, (s + 1) % 2)
                        if w == 9:
                            route_silu(t0 + s + 1)
                        if w == 17:
                            copy_weights(t0 + s + 1)
                    if attention:
                        attention_stage(u, p - ATT0)

            act.wait_ge(const_seq, 2)
            act.activation(warm[:, :], half[:, 0:1], ACT.Silu)
            act.wait_ge(setup_psum, 1)
            act.copy(RT[:, :], attP[:, 3 * P:3 * P + E]).then_inc(setup_sb, 1)
            normalise(0, 0, 0)
            normalise(0, 0, 1)
            next_high(0, 0)
            for unit in range(SHARED):
                split_high(unit)
            route_silu(0)
            for unit in range(SHARED, AHEAD):
                split_high(unit)
            pair(0, True, False, False)
            for p in range(1, ATT0):
                pair(p, False, False, False)
            with act.Fori(ATT0, ATT1) as p:
                pair(p, False, True, False)
            for p in range(ATT1, LAST):
                pair(p, False, False, False)
            pair(LAST, False, False, True)

        @block.vector
        def _(dve):
            def merge_stats(seq, base, halves, nmean_out, var_out, tmp):
                dve.wait_ge(seq, base + 1)
                dve.tensor_tensor(tmp[:, 0, :], halves[:, :, 1], halves[:, :, 4], ALU.add)
                dve.tensor_tensor(tmp[:, 1, :], halves[:, :, 1], halves[:, :, 4], ALU.subtract)
                dve.tensor_tensor(tmp[:, 2, :], halves[:, :, 2], halves[:, :, 5], ALU.add).then_inc(seq, 1)
                dve.wait_ge(seq, base + 2)
                dve.tensor_scalar(nmean_out, tmp[:, 0, :], -0.5, None, ALU.mult)
                dve.scalar_tensor_tensor(tmp[:, 3, :], tmp[:, 1, :], 0.25, tmp[:, 1, :], ALU.mult, ALU.mult)
                dve.tensor_scalar(tmp[:, 4, :], tmp[:, 2, :], 1.0 / P, EPS, ALU.mult,
                                  ALU.add).then_inc(seq, 1)
                dve.wait_ge(seq, base + 3)
                dve.tensor_tensor(var_out, tmp[:, 3, :], tmp[:, 4, :], ALU.add).then_inc(seq, 1)

            def split_low(unit):
                dve.wait_ge(w_hi_done, unit + 1)
                dve.tensor_tensor(W_lo[:, unit, :, :], W_in[:, unit, :, :],
                                  W_hi[:, unit, :, :].bitcast(F32), ALU.subtract).then_inc(w_lo_late, 1)

            def stats(t, blk):
                for j in range(TILES):
                    ins = dve.bn_stats(bst[:, j, :], X[:, bass.ds(blk * TILES + j, 1), :]
                                       .rearrange("p o d -> p (o d)"))
                ins.then_inc(stats_seq, 1)
                merge_stats(stats_seq, 4 * t, bst, nmean[:, :], vareps[:, :], parts)

            def next_full(t):
                dve.wait_ge(xt_done, t + 1)
                if not (isinstance(t, int) and t == 0):
                    dve.wait_ge(xt_lo_ready, t)
                dve.tensor_copy(XT[:, :], prepP[:, :]).then_inc(xt_ready, 1)

            G16 = TILES * GROUPS
            comb_v = comb[:, 0:E * TILES].rearrange("p (e j) -> p j e", j=TILES)

            def route(t, part):
                base = ROUTE_OPS * t
                sel4 = sel[:, :, :].rearrange("p t (g i) -> p (t g) i", i=PER_GROUP)
                if part == 0:
                    dve.wait_ge(logits_done, t + 1)
                    flat = prepP[:, 0:TILES * E]
                    near_f = near[:, :, :].rearrange("p t e -> p (t e)")
                    dve.tensor_scalar(near_f, flat, -NEAR_ZERO, None, ALU.is_gt).then_inc(route_seq, 1)
                    dve.wait_ge(route_seq, base + 1)
                    dve.scalar_tensor_tensor(near_f, flat, NEAR_ZERO, near_f, ALU.is_lt,
                                             ALU.mult).then_inc(route_seq, 1)
                    dve.wait_ge(route_seq, base + 2)
                    dve.scalar_tensor_tensor(lg[:, :, :].rearrange("p t e -> p (t e)"), near_f, NEAR_ZERO,
                                             flat, ALU.mult, ALU.add).then_inc(route_seq, 1)
                    dve.wait_ge(route_seq, base + 3)
                    dve.reciprocal(rcl[:, :, :], lg[:, :, :]).then_inc(route_seq, 1)
                if part == 1:
                    dve.wait_ge(silu_route, t + 1)
                    dve.wait_ge(route_seq, base + 4)
                    dve.tensor_tensor(score[:, :, :], sil[:, :, :], rcl[:, :, :],
                                      ALU.mult).then_inc(route_seq, 1)
                    dve.wait_ge(route_seq, base + 5)
                    dve.tensor_tensor(sel[:, :, :], score[:, :, :], ebias[:, :, :],
                                      ALU.add).then_inc(route_seq, 1)
                    dve.wait_ge(route_seq, base + 6)
                    dve.tensor_tensor(hi2[:, :, :], sel4[:, :, 0:2], sel4[:, :, 2:4],
                                      ALU.max).then_inc(route_seq, 1)
                    dve.tensor_tensor(lo2[:, :, :], sel4[:, :, 0:2], sel4[:, :, 2:4],
                                      ALU.min).then_inc(route_seq, 1)
                if part == 2:
                    dve.wait_ge(route_seq, base + 8)
                    dve.tensor_tensor(top1[:, :], hi2[:, :, 0], hi2[:, :, 1], ALU.max).then_inc(route_seq, 1)
                    dve.tensor_tensor(mid[:, :], hi2[:, :, 0], hi2[:, :, 1], ALU.min).then_inc(route_seq, 1)
                    dve.tensor_tensor(low1[:, :], lo2[:, :, 0], lo2[:, :, 1], ALU.max).then_inc(route_seq, 1)
                    dve.wait_ge(route_seq, base + 11)
                    dve.tensor_tensor(mid[:, :], mid[:, :], low1[:, :], ALU.max).then_inc(route_seq, 1)
                    dve.wait_ge(route_seq, base + 12)
                    dve.tensor_tensor(gsc[:, :, :].rearrange("p t g -> p (t g)"), top1[:, :], mid[:, :],
                                      ALU.add).then_inc(route_seq, 1)
                if part == 3:
                    dve.wait_ge(route_seq, base + 13)
                    other = gsc[:, :, :].unsqueeze(2).broadcast_to([P, TILES, GROUPS, GROUPS])
                    own = gsc[:, :, :].unsqueeze(3).broadcast_to([P, TILES, GROUPS, GROUPS])
                    dve.tensor_tensor(gt[:, :, :, :], other, own, ALU.is_gt).then_inc(route_seq, 1)
                    dve.tensor_tensor(eq[:, :, :, :], other, own, ALU.is_equal).then_inc(route_seq, 1)
                    dve.wait_ge(route_seq, base + 15)
                    dve.tensor_tensor(eq[:, :, :, :], eq[:, :, :, :], before[:, :, :, :],
                                      ALU.mult).then_inc(route_seq, 1)
                    dve.wait_ge(route_seq, base + 16)
                    dve.tensor_tensor(gt[:, :, :, :], gt[:, :, :, :], eq[:, :, :, :],
                                      ALU.add).then_inc(route_seq, 1)
                    dve.wait_ge(route_seq, base + 17)
                    dve.tensor_reduce(grank[:, :], gt[:, :, :, :].rearrange("p t g h -> p (t g) h"),
                                      AX.X, ALU.add).then_inc(route_seq, 1)
                if part == 4:
                    dve.wait_ge(route_seq, base + 18)
                    dve.tensor_scalar(gmask[:, :], grank[:, :], float(TOP_GROUPS), None,
                                      ALU.is_lt).then_inc(route_seq, 1)
                    dve.wait_ge(route_seq, base + 19)
                    gm = gmask[:, :].unsqueeze(2).broadcast_to([P, G16, PER_GROUP])
                    pk = picked[:, :, :].rearrange("p t (g i) -> p (t g) i", i=PER_GROUP)
                    mk = masked[:, :, :].rearrange("p t (g i) -> p (t g) i", i=PER_GROUP)
                    dve.tensor_tensor(pk, sel4, gm, ALU.mult).then_inc(route_seq, 1)
                    dve.wait_ge(route_seq, base + 20)
                    dve.scalar_tensor_tensor(mk, gm, -1.0, pk, ALU.add, ALU.add).then_inc(route_seq, 1)
                if part == 5:
                    for j in range(TILES):
                        ins = dve.max(top8[:, j, :], masked[:, j, :])
                    ins.then_inc(route_seq, 1)
                if part == 6:
                    for j in range(TILES):
                        ins = dve.max_index(idx8[:, j, :], top8[:, j, :], masked[:, j, :])
                    ins.then_inc(route_seq, 1)
                    dve.wait_ge(route_seq, base + 23)
                    places = idx8[:, :, 0:TOP_K].unsqueeze(2).broadcast_to([P, TILES, E, TOP_K])
                    dve.tensor_tensor(hot[:, :, :, :], enum[:, :, :, :], places,
                                      ALU.is_equal).then_inc(route_seq, 1)
                if part == 7:
                    dve.wait_ge(route_seq, base + 24)
                    dve.tensor_reduce(emask[:, :, :], hot[:, :, :, :], AX.X, ALU.add).then_inc(route_seq, 1)
                    dve.wait_ge(route_seq, base + 25)
                    dve.tensor_tensor(wsel[:, :, :], emask[:, :, :], score[:, :, :],
                                      ALU.mult).then_inc(route_seq, 1)
                    dve.wait_ge(route_seq, base + 26)
                    dve.tensor_reduce(wsum[:, :], wsel[:, :, :], AX.X, ALU.add).then_inc(norm_seq, 1)
                    dve.wait_ge(norm_seq, 3 * t + 1)
                    dve.tensor_scalar(wsum[:, :], wsum[:, :], 1e-20, None, ALU.add).then_inc(norm_seq, 1)
                    dve.wait_ge(norm_seq, 3 * t + 2)
                    dve.reciprocal(wrec[:, :], wsum[:, :]).then_inc(norm_seq, 1)
                    dve.wait_ge(norm_seq, 3 * t + 3)
                    rec = wrec[:, :].unsqueeze(2).broadcast_to([P, TILES, E])
                    dve.scalar_tensor_tensor(comb_v, wsel[:, :, :], ROUTED_SCALE, rec,
                                             ALU.mult, ALU.mult).then_inc(route_seq, 1)

            def residual(t, blk):
                dve.wait_ge(y_back, t + 1)
                xb = X[:, bass.ds(blk * TILES, TILES), :].rearrange("p j d -> p (j d)")
                dve.scalar_tensor_tensor(xb, backP[:, :], 0.5, xb, ALU.mult,
                                         ALU.add).then_inc(x_updated, 1)

            def attention_stage(u, b):
                v = ATT_OPS * b
                if 1 <= u <= 4:
                    j0 = 2 * (u - 1)
                    if u == 1:
                        dve.wait_ge(x_updated, 2 * b + 2)
                    for j in (j0, j0 + 1):
                        ins = dve.bn_stats(ast[:, j, :], X[:, bass.ds(b * BT + j, 1), :]
                                           .rearrange("p o d -> p (o d)"))
                    if u == 4:
                        ins.then_inc(att_seq, 1)
                        merge_stats(att_seq, v, ast, anmean[:, :], avar[:, :], aparts)
                if u == 14:
                    dve.wait_ge(att_act, 6 * b + 1)
                    dve.tensor_scalar(s_row[:, :], ones[:, :], GS[:, P:P + 1], None,
                                      ALU.mult).then_inc(att_seq, 1)
                    dve.tensor_scalar(Gc[:, P:P + 1], GS[:, P:P + 1], 1.0 / SEQ, None, ALU.mult)
                    dve.tensor_scalar(nmu[:, :], GS[:, P:P + 1], -1.0 / SEQ / SEQ, None, ALU.mult)
                    dve.tensor_scalar(Gn[:, :], GS[:, 0:P], 1.0 / SEQ, None, ALU.mult).then_inc(att_seq, 1)
                if u == 17:
                    dve.wait_ge(att_pe, 12 * b + 4)
                    dve.wait_ge(att_seq, v + 6)
                    dve.scalar_tensor_tensor(P1[:, :], bvb[:, :], GS[:, P:P + 1], attP[:, 0:P],
                                             ALU.mult, ALU.add)
                    dve.scalar_tensor_tensor(rv[:, :], bvb[:, :], float(SEQ), attP[:, P:2 * P],
                                             ALU.mult, ALU.add).then_inc(att_seq, 1)
                    dve.scalar_tensor_tensor(Gc[:, 0:P], attP[:, 2 * P:3 * P], nmu[:, :], Gn[:, :],
                                             ALU.mult, ALU.add).then_inc(att_seq, 1)
                if u == 20:
                    dve.wait_ge(att_pe, 12 * b + 5)
                    dve.scalar_tensor_tensor(Mf[:, :], rv[:, :], bk[:, :], attP[:, 0:P],
                                             ALU.mult, ALU.add).then_inc(att_seq, 1)
                    dve.wait_ge(att_seq, v + 9)
                    dve.tensor_tensor(Mm[:, :], Mf[:, :], blk1[:, :], ALU.mult).then_inc(att_seq, 1)
                if u == 24:
                    dve.wait_ge(att_pe, 12 * b + 7)
                    dve.wait_ge(att_act, 6 * b + 5)
                    dve.tensor_tensor(quad[:, :], attP[:, 0:P], AT[:, 0:P], ALU.mult).then_inc(att_seq, 1)
                    dve.tensor_tensor(chmean[:, :], attP[:, P:P + 1], AT[:, P:P + 1],
                                      ALU.add).then_inc(att_seq, 1)
                if u == 27:
                    dve.wait_ge(att_seq, v + 12)
                    dve.tensor_reduce(chvar[:, :], quad[:, :], AX.X, ALU.add)
                    dve.wait_ge(att_pe, 12 * b + 8)
                    dve.tensor_copy(gmean[:, :], attP[:, 2 * P:2 * P + 1])
                    dve.tensor_tensor(dev[:, :], chmean[:, :], attP[:, 2 * P:2 * P + 1],
                                      ALU.subtract).then_inc(att_seq, 1)
                    dve.wait_ge(att_seq, v + 13)
                    dve.scalar_tensor_tensor(dev2[:, :], dev[:, :], dev[:, :], chvar[:, :],
                                             ALU.mult, ALU.add).then_inc(att_seq, 1)
                if u == 30:
                    dve.wait_ge(att_pe, 12 * b + 9)
                    dve.tensor_scalar(gvar[:, :], attP[:, 3 * P:3 * P + 1], EPS, None,
                                      ALU.add).then_inc(att_seq, 1)
                if u == 31:
                    dve.wait_ge(att_pow, 3 * b + 3)
                    dve.tensor_tensor(gsc1[:, :], grstd[:, :], gw[:, :], ALU.mult).then_inc(att_seq, 1)
                    dve.wait_ge(att_seq, v + 16)
                    dve.tensor_tensor(gms[:, :], gmean[:, :], gsc1[:, :], ALU.mult)
                    dve.tensor_scalar(ATs[:, :], AT[:, 0:P], gsc1[:, :], None, ALU.mult).then_inc(att_seq, 1)
                    dve.wait_ge(att_seq, v + 17)
                    dve.tensor_tensor(gsh[:, :], gb[:, :], gms[:, :], ALU.subtract).then_inc(att_seq, 1)
                    dve.wait_ge(att_seq, v + 18)
                    dve.scalar_tensor_tensor(z1[:, :], AT[:, P:P + 1], gsc1[:, :], gsh[:, :],
                                             ALU.mult, ALU.add).then_inc(z_ready, 1)
                    dve.wait_ge(z_ready, b + 1)
                    dve.tensor_scalar(zb[:, :], ones[:, :], z1[:, :], None, ALU.mult).then_inc(att_seq, 1)
                if u == 33:
                    dve.wait_ge(att_pe, 12 * b + 10)
                    dve.wait_ge(att_act, 6 * b + 6)
                    dve.tensor_tensor(brow[:, :], attP[:, P:2 * P], bob[:, :], ALU.add).then_inc(att_seq, 1)
                if u == 34:
                    dve.wait_ge(att_seq, v + 20)
                    for g in range(BT // TILES):
                        xb = X[:, bass.ds(b * BT + g * TILES, TILES), :]
                        dve.tensor_tensor(xb, xb, brow[:, :].unsqueeze(1).broadcast_to([P, TILES, P]),
                                          ALU.add).then_inc(row_added, 1)
                if u == 35:
                    for g, bank in enumerate((attP, backP)):
                        xb = X[:, bass.ds(b * BT + g * TILES, TILES), :].rearrange("p j d -> p (j d)")
                        dve.wait_ge(att_pe, 12 * b + 11 + g)
                        dve.wait_ge(row_added, 2 * b + 1 + g)
                        dve.tensor_tensor(xb, bank[:, :], xb, ALU.add).then_inc(attended, 1)

            def weight(p, u, first):
                n, w, s = PAIR * p, u % UNITS, u // UNITS
                if w < SHARED or w in POOL_WEIGHTED:
                    return
                e = w - SHARED
                dve.wait_ge(mul_done, n + u + 1)
                if e % CSEM == 0 or w - 1 in POOL_WEIGHTED:
                    dve.wait_ge(cb_in[e // CSEM], 16 * (2 * p + s + 1))
                if not (first and u < SLOTS):
                    dve.wait_ge(low_done, n + u + 1 - SLOTS)
                dve.tensor_tensor(A[:, u % SLOTS, :], SU[:, u % SUS, :], CB[:, e, :],
                                  ALU.mult).then_inc(weighted, 1)

            def pair(p, first, attention, last):
                n, t0 = PAIR * p, 2 * p
                for u in range(PAIR):
                    w, s = u % UNITS, u // UNITS
                    if w in (13, 14) and not (last and s == 1):
                        dve.wait_ge(route_seq, ROUTE_OPS * (t0 + s + 1) + (21 if w == 13 else 22))
                    late = first and u == SHARED + 1
                    if not (first and u == 0) and not late:
                        weight(p, u - 1, first)
                    dve.wait_ge(silu_done, n + u + 1)
                    dve.wait_ge(up_done, n + u + 1)
                    if w < SHARED:
                        if not (first and u < SLOTS):
                            dve.wait_ge(low_done, n + u + 1 - SLOTS)
                        dst = A[:, u % SLOTS, :]
                    else:
                        if (w - SUS) in POOL_WEIGHTED:
                            dve.wait_ge(*weighted_by(t0 + s, w - SUS))
                        dst = SU[:, u % SUS, :]
                    dve.tensor_tensor(dst, upP[u % 2][:, :], S[:, u % 2, :], ALU.mult).then_inc(mul_done, 1)
                    if late:
                        weight(p, u - 1, first)
                    if w == 7 and not (first and s == 0):
                        residual(t0 + s - 1, 2 * ((p - 1 + s) % BATCH) + (1 - s))
                    if not (last and s == 1):
                        t, blk = t0 + s + 1, 2 * ((p + s) % BATCH) + (1 - s)
                        if w == 0:
                            if first and s == 0:
                                dve.wait_ge(x_rest, 16 * BATCH)
                            if not first:
                                dve.wait_ge(mul_done, n)
                            stats(t, blk)
                        if w == 6:
                            next_full(t)
                        if 8 <= w < 16:
                            route(t, w - 8)
                    if first and u + AHEAD < UNITS:
                        split_low(u + AHEAD)
                    if attention:
                        attention_stage(u, p - ATT0)

            dve.memset(comb[:, :], 0.0)
            dve.wait_ge(x_first, 16)
            stats(0, 0)
            next_full(0)
            dve.wait_ge(router_in, 32)
            dve.wait_ge(const_seq, CONSTS)
            dve.wait_ge(xt_hi_ready, 1)
            dve.tensor_tensor(XT_lo[:, 0, :], XT[:, :], XT_hi[:, 0, :].bitcast(F32),
                              ALU.subtract).then_inc(xt_lo_ready, 1)
            dve.tensor_scalar(blkm[:, :], blk1[:, :], 1.0 / HEAD, None, ALU.mult).then_inc(attended, 2)
            for part in range(8):
                if part in (5, 6):
                    dve.wait_ge(route_seq, 21 if part == 5 else 22)
                route(0, part)
            pair(0, True, False, False)
            for p in range(1, ATT0):
                pair(p, False, False, False)
            with dve.Fori(ATT0, ATT1) as p:
                pair(p, False, True, False)
            for p in range(ATT1, LAST):
                pair(p, False, False, False)
            pair(LAST, False, False, True)
            weight(LAST, PAIR - 1, False)
            residual(STEPS - 1, NBLK - 1)


_INS = ["L0_attn_x", "L0_attn_Wqkv_w", "L0_attn_Wqkv_b", "L0_attn_gn_w", "L0_attn_gn_b",
        "L0_attn_out_w", "L0_attn_out_b", "L0_ffn_router_w", "L0_ffn_bias", "L0_ffn_gate_w",
        "L0_ffn_up_w", "L0_ffn_down_w", "L0_ffn_sh_gate_w", "L0_ffn_sh_up_w", "L0_ffn_sh_down_w"]
_OUTS = [((4, 1024, 128), "float32")]


def kernel(**inputs):
    import numpy as _np
    import concourse.bacc as _bacc
    from concourse import mybir as _mybir
    from concourse.bass_utils import run_bass_kernel_spmd as _run

    nc = _bacc.Bacc("TRN2", target_bir_lowering=False, num_devices=1)
    arrays, args = {}, []
    for name in _INS:
        a = _np.ascontiguousarray(inputs[name])
        arrays[f"in_{name}_dram"] = a
        args.append(nc.dram_tensor(f"in_{name}_dram", a.shape, _mybir.dt.from_np(a.dtype), kind="ExternalInput").ap())
    for i, (shape, dtype) in enumerate(_OUTS):
        dt = _mybir.dt.from_np(_np.dtype(dtype))
        args.append(nc.dram_tensor(f"out_{i}_dram", shape, dt, kind="ExternalOutput").ap())
    macaron_kernel(nc, *args)
    r = _run(nc, [arrays], core_ids=[0])
    got = tuple(r.results[0][f"out_{i}_dram"] for i in range(len(_OUTS)))
    return got[0]
```
